# Optimizing a Trainium2 kernel written in Bass

```python
import numpy as np
import jax
import jax.numpy as jnp

def _softmax(x, axis=-1):
    return jax.nn.softmax(x, axis=axis)

def _gelu(x):
    return jax.nn.gelu(x, approximate=True)

def _silu(x):
    return jax.nn.silu(x)

def _sigmoid(x):
    return jax.nn.sigmoid(x)

def _layernorm(x, axis=-1, eps=1e-05):
    m = jnp.mean(x, axis=axis, keepdims=True)
    v = jnp.var(x, axis=axis, keepdims=True)
    return (x - m) / jnp.sqrt(v + eps)

def _scatter_add(tgt, idx, src, axis=0):
    return tgt.at[idx].add(src)

def _segment_sum(src, seg, n):
    return jax.ops.segment_sum(src, seg, n)
kernel_name = 'mk_prb_d1_jaxref_r4_5b2987'

def setup_inputs(seed: int=0):
    np.random.seed(seed)
    _w = jnp.asarray

    def _L0_attn_setup():
        import jax, jax.numpy as jnp
        import numpy as np
        from jax import lax
        H = 64
        P = 64
        N = 128
        G = 8
        K = 4
        D_MODEL = 1024
        I = H * P
        GN = G * N
        CONV_DIM = I + 2 * GN
        PROJ = I + CONV_DIM + H
        EPS = 1e-05
        GROUP_SIZE = I // G

        def _reference_tuple_inner(hidden_states, in_proj_w, conv_weight, conv_bias, dt_bias, A_log, D, norm_weight, out_proj_w):
            B, L, _ = hidden_states.shape
            proj = jnp.einsum('bld,pd->blp', hidden_states, in_proj_w)
            gate = proj[..., :I]
            hbc = proj[..., I:I + CONV_DIM]
            dt = proj[..., -H:]
            pad = jnp.pad(hbc, ((0, 0), (K - 1, 0), (0, 0)))
            conv = conv_bias
            for k in range(K):
                conv = conv + pad[:, k:k + L, :] * conv_weight[:, k]
            xBC = jax.nn.silu(conv)
            x = xBC[..., :I].reshape(B, L, H, P)
            Bm = xBC[..., I:I + GN].reshape(B, L, G, N)
            Cm = xBC[..., I + GN:].reshape(B, L, G, N)
            hpg = H // G
            B_h = jnp.repeat(Bm, hpg, axis=2)
            C_h = jnp.repeat(Cm, hpg, axis=2)
            dt_p = jax.nn.softplus(dt + dt_bias)
            A = -jnp.exp(A_log)
            dA = jnp.exp(dt_p * A)
            dtx = dt_p[..., None] * x

            def step(state, inp):
                dA_t, dtx_t, B_t, C_t = inp
                state = state * dA_t[..., None, None] + dtx_t[..., None] * B_t[:, :, None, :]
                y_t = jnp.einsum('bhpn,bhn->bhp', state, C_t)
                return (state, y_t)
            xs = (jnp.moveaxis(dA, 1, 0), jnp.moveaxis(dtx, 1, 0), jnp.moveaxis(B_h, 1, 0), jnp.moveaxis(C_h, 1, 0))
            state0 = jnp.zeros((B, H, P, N), jnp.float32)
            final_state, ys = lax.scan(step, state0, xs)
            y = jnp.moveaxis(ys, 0, 1) + x * D[None, None, :, None]
            y = y.reshape(B, L, I)
            yg = y.reshape(B, L, G, GROUP_SIZE)
            var = jnp.mean(yg * yg, axis=-1, keepdims=True)
            yn = (yg * lax.rsqrt(var + EPS)).reshape(B, L, I) * norm_weight
            yn = yn * jax.nn.silu(gate)
            out = jnp.einsum('bli,di->bld', yn, out_proj_w)
            conv_state_new = jnp.moveaxis(hbc[:, L - (K - 1):, :], 1, 2)
            return (out, conv_state_new, final_state)
        key = jax.random.key(seed)
        ks = jax.random.split(key, 6)
        B, L = (2, 512)
        s = 0.02
        return {'hidden_states': jax.random.normal(ks[0], (B, L, D_MODEL), jnp.float32), 'in_proj_w': jax.random.normal(ks[1], (PROJ, D_MODEL), jnp.float32) * s, 'conv_weight': jax.random.normal(ks[2], (CONV_DIM, K), jnp.float32) * s, 'conv_bias': jnp.zeros((CONV_DIM,), jnp.float32), 'dt_bias': jnp.ones((H,), jnp.float32), 'A_log': jnp.log(jnp.arange(1, H + 1, dtype=jnp.float32)), 'D': jnp.ones((H,), jnp.float32), 'norm_weight': jnp.ones((I,), jnp.float32), 'out_proj_w': jax.random.normal(ks[3], (D_MODEL, I), jnp.float32) * s}
    _L0_attn_in = _L0_attn_setup()

    def _L0_ffn_setup():
        import jax, jax.numpy as jnp
        import numpy as np

        def sparsemax(z):
            E = z.shape[-1]
            z_sorted = -jnp.sort(-z, axis=-1)
            z_cum = jnp.cumsum(z_sorted, axis=-1)
            k = jnp.arange(1, E + 1, dtype=z.dtype)
            support = 1.0 + k * z_sorted > z_cum
            k_z = jnp.sum(support, axis=-1, keepdims=True)
            tau_sum = jnp.take_along_axis(z_cum, k_z.astype(jnp.int32) - 1, axis=-1)
            tau = (tau_sum - 1.0) / k_z.astype(z.dtype)
            return jnp.maximum(z - tau, 0.0)
        key = jax.random.key(seed)
        ks = jax.random.split(key, 6)
        B, S, D_IN, D_OUT, E, R = (8, 512, 1024, 1024, 8, 16)
        x = jax.random.normal(ks[0], (B, S, D_IN), dtype=jnp.float32)
        W_base = jax.random.normal(ks[1], (D_OUT, D_IN), dtype=jnp.float32) * D_IN ** (-0.5)
        b_base = jax.random.normal(ks[2], (D_OUT,), dtype=jnp.float32) * 0.01
        W_router = jax.random.normal(ks[3], (E, D_IN), dtype=jnp.float32) * D_IN ** (-0.5)
        b_router = jnp.zeros((E,), dtype=jnp.float32)
        lora_A = jax.random.normal(ks[4], (E, D_IN, R), dtype=jnp.float32) * D_IN ** (-0.5)
        lora_B = jnp.zeros((E, R, D_OUT), dtype=jnp.float32)
        return {'x': x, 'W_base': W_base, 'b_base': b_base, 'W_router': W_router, 'b_router': b_router, 'lora_A': lora_A, 'lora_B': lora_B}
    _L0_ffn_in = _L0_ffn_setup()
    _d = {'L0_attn_hidden_states': _L0_attn_in['hidden_states'], 'L0_attn_in_proj_w': _L0_attn_in['in_proj_w'], 'L0_attn_conv_weight': _L0_attn_in['conv_weight'], 'L0_attn_conv_bias': _L0_attn_in['conv_bias'], 'L0_attn_dt_bias': _L0_attn_in['dt_bias'], 'L0_attn_A_log': _L0_attn_in['A_log'], 'L0_attn_D': _L0_attn_in['D'], 'L0_attn_norm_weight': _L0_attn_in['norm_weight'], 'L0_attn_out_proj_w': _L0_attn_in['out_proj_w'], 'L0_ffn_W_base': _L0_ffn_in['W_base'], 'L0_ffn_b_base': _L0_ffn_in['b_base'], 'L0_ffn_W_router': _L0_ffn_in['W_router'], 'L0_ffn_b_router': _L0_ffn_in['b_router'], 'L0_ffn_lora_A': _L0_ffn_in['lora_A'], 'L0_ffn_lora_B': _L0_ffn_in['lora_B']}
    _x0 = _d['L0_attn_hidden_states']
    _d['L0_attn_hidden_states'] = jax.random.normal(jax.random.fold_in(jax.random.key(seed), 1), (1, 2048, 1024), dtype=_x0.dtype)
    del _x0
    return _d

def reference(L0_attn_hidden_states, L0_attn_in_proj_w, L0_attn_conv_weight, L0_attn_conv_bias, L0_attn_dt_bias, L0_attn_A_log, L0_attn_D, L0_attn_norm_weight, L0_attn_out_proj_w, L0_ffn_W_base, L0_ffn_b_base, L0_ffn_W_router, L0_ffn_b_router, L0_ffn_lora_A, L0_ffn_lora_B):

    def _L0_attn_ref(hidden_states, in_proj_w, conv_weight, conv_bias, dt_bias, A_log, D, norm_weight, out_proj_w):
        import jax, jax.numpy as jnp
        import numpy as np
        from jax import lax
        H = 64
        P = 64
        N = 128
        G = 8
        K = 4
        D_MODEL = 1024
        I = H * P
        GN = G * N
        CONV_DIM = I + 2 * GN
        PROJ = I + CONV_DIM + H
        EPS = 1e-05
        GROUP_SIZE = I // G

        def _reference_tuple_inner(hidden_states, in_proj_w, conv_weight, conv_bias, dt_bias, A_log, D, norm_weight, out_proj_w):
            B, L, _ = hidden_states.shape
            proj = jnp.einsum('bld,pd->blp', hidden_states, in_proj_w)
            gate = proj[..., :I]
            hbc = proj[..., I:I + CONV_DIM]
            dt = proj[..., -H:]
            pad = jnp.pad(hbc, ((0, 0), (K - 1, 0), (0, 0)))
            conv = conv_bias
            for k in range(K):
                conv = conv + pad[:, k:k + L, :] * conv_weight[:, k]
            xBC = jax.nn.silu(conv)
            x = xBC[..., :I].reshape(B, L, H, P)
            Bm = xBC[..., I:I + GN].reshape(B, L, G, N)
            Cm = xBC[..., I + GN:].reshape(B, L, G, N)
            hpg = H // G
            B_h = jnp.repeat(Bm, hpg, axis=2)
            C_h = jnp.repeat(Cm, hpg, axis=2)
            dt_p = jax.nn.softplus(dt + dt_bias)
            A = -jnp.exp(A_log)
            dA = jnp.exp(dt_p * A)
            dtx = dt_p[..., None] * x

            def step(state, inp):
                dA_t, dtx_t, B_t, C_t = inp
                state = state * dA_t[..., None, None] + dtx_t[..., None] * B_t[:, :, None, :]
                y_t = jnp.einsum('bhpn,bhn->bhp', state, C_t)
                return (state, y_t)
            xs = (jnp.moveaxis(dA, 1, 0), jnp.moveaxis(dtx, 1, 0), jnp.moveaxis(B_h, 1, 0), jnp.moveaxis(C_h, 1, 0))
            state0 = jnp.zeros((B, H, P, N), jnp.float32)
            final_state, ys = lax.scan(step, state0, xs)
            y = jnp.moveaxis(ys, 0, 1) + x * D[None, None, :, None]
            y = y.reshape(B, L, I)
            yg = y.reshape(B, L, G, GROUP_SIZE)
            var = jnp.mean(yg * yg, axis=-1, keepdims=True)
            yn = (yg * lax.rsqrt(var + EPS)).reshape(B, L, I) * norm_weight
            yn = yn * jax.nn.silu(gate)
            out = jnp.einsum('bli,di->bld', yn, out_proj_w)
            conv_state_new = jnp.moveaxis(hbc[:, L - (K - 1):, :], 1, 2)
            return (out, conv_state_new, final_state)
        return _reference_tuple_inner(hidden_states, in_proj_w, conv_weight, conv_bias, dt_bias, A_log, D, norm_weight, out_proj_w)[0]

    def _L0_ffn_ref(x, W_base, b_base, W_router, b_router, lora_A, lora_B):
        import jax, jax.numpy as jnp
        import numpy as np

        def sparsemax(z):
            E = z.shape[-1]
            z_sorted = -jnp.sort(-z, axis=-1)
            z_cum = jnp.cumsum(z_sorted, axis=-1)
            k = jnp.arange(1, E + 1, dtype=z.dtype)
            support = 1.0 + k * z_sorted > z_cum
            k_z = jnp.sum(support, axis=-1, keepdims=True)
            tau_sum = jnp.take_along_axis(z_cum, k_z.astype(jnp.int32) - 1, axis=-1)
            tau = (tau_sum - 1.0) / k_z.astype(z.dtype)
            return jnp.maximum(z - tau, 0.0)
        base_out = jnp.einsum('bsd,od->bso', x, W_base) + b_base
        logits = jnp.einsum('bsd,ed->bse', x, W_router) + b_router
        weights = sparsemax(logits)
        h = jnp.einsum('bsd,edr->bser', x, lora_A)
        expert_out = jnp.einsum('bser,bse,ero->bso', h, weights, lora_B)
        return base_out + expert_out
    x = L0_attn_hidden_states
    xn = _layernorm(x, axis=-1)
    x = x + _L0_attn_ref(xn, L0_attn_in_proj_w, L0_attn_conv_weight, L0_attn_conv_bias, L0_attn_dt_bias, L0_attn_A_log, L0_attn_D, L0_attn_norm_weight, L0_attn_out_proj_w) + _L0_ffn_ref(xn, L0_ffn_W_base, L0_ffn_b_base, L0_ffn_W_router, L0_ffn_b_router, L0_ffn_lora_A, L0_ffn_lora_B)
    return x

_drawn_inputs = setup_inputs


def setup_inputs(seed=0):
    import zlib

    import numpy as np

    out = dict(_drawn_inputs(seed))
    spreads = {'L0_attn_conv_bias': (0.0, 0.1),
     'L0_attn_dt_bias': (1.0, 0.6),
     'L0_attn_D': (1.0, 0.2),
     'L0_attn_norm_weight': (1.0, 0.2),
     'L0_ffn_b_router': (0.0, 0.602),
     'L0_ffn_lora_B': (0.0, 0.1)}
    factors = {'L0_attn_A_log': 8.0, 'L0_ffn_b_base': 8.0}
    for name, (base, spread) in spreads.items():
        noise = np.random.default_rng([zlib.crc32(name.encode()), seed]).standard_normal(out[name].shape)
        drawn = base * np.exp(spread * noise) if base else spread * noise
        out[name] = jnp.asarray(drawn.astype(out[name].dtype))
    for name, factor in factors.items():
        out[name] = (out[name] * factor).astype(out[name].dtype)
    return out
```

```python
from contextlib import ExitStack

import concourse.bass as bass
from concourse import mybir

F32 = mybir.dt.float32
F16 = mybir.dt.float16
BF16 = mybir.dt.bfloat16
I32 = mybir.dt.int32
ALU = mybir.AluOpType
ACT = mybir.ActivationFunctionType
AX = mybir.AxisListType

P = 128
L = 2048
DM = 1024
KT = DM // P
H, HD, NS, G = 64, 64, 128, 8
HG = H // G
GC = HG * HD
XT = GC // P
TAPS = 4
NCT = XT + 2
NU = NCT + 4
ST = 512
NC = ST // P
CHUNKS = L // P
HALF = L // 2
STEPS = 2 * G
E, R = 8, 16
ER = E * R
AUX = H + E + ER
EPS = 1e-5
SCALE = 64.0
LN_POW = -0.5
OUT_POW2 = SCALE ** 4
A_DT, A_W, A_ELA, A_ETOT, A_NLA = range(5)
REC_D = 5 * NC * HG
REC_NW = REC_D + HG
REC_LA = REC_NW + XT
PARTS = 3
LAW = PARTS * HG
REC = REC_LA + NC * LAW // 2
C_ID, C_LE, C_GT, C_NEG, C_HOT, C_K = 0, P, 2 * P, 3 * P, 4 * P, 4 * P + HG * P
CST = C_K + E
CW = NCT * (TAPS + 1)


def at_least(engine, sem, value):
    if isinstance(value, int) and value <= 0:
        return
    engine.wait_ge(sem, value)


def prologue(nc, ext, d, keep):
    xn, Wb, ident32, stage = keep["xn"], keep["W"], keep["ident32"], keep["stage"]
    ORDER = [2, 3, 0, 1]
    rows = [T * NC + c for T in ORDER for c in range(NC)]
    NF = KT + 3
    with ExitStack() as ctx:
        def sb(name, shape, dt=F32):
            return ctx.enter_context(nc.sbuf_tensor("p_" + name, shape, dt))

        def sem(name):
            return ctx.enter_context(nc.semaphore("p_" + name))

        xrow = sb("xrow", [P, 2, DM])
        xnrow = sb("xnrow", [P, DM])
        orow = sb("orow", [P, 2, DM])
        bbase = sb("bbase", [P, DM])
        bias_row = sb("bias_row", [P, H + E])
        alog = sb("alog", [P, H])
        expa = sb("expa", [P, H])
        dvec = sb("dvec", [P, H])
        nwall = sb("nwall", [P, G * XT])
        cst = sb("cst", [P, CST])
        onesf = sb("onesf", [P, P])
        stats = sb("stats", [P, 2, 6])
        mv = sb("mv", [P, 2])
        veps = sb("veps", [P, 1])
        rstd = sb("rstd", [P, 1])
        mhalf = sb("mhalf", [P, 1])
        aux = sb("aux", [P, AUX])
        dtraw = sb("dtraw", [P, CHUNKS, H])
        zs = sb("zs", [P, E])
        cum = sb("cum", [P, 2, E])
        kz = sb("kz", [P, E])
        sup = sb("sup", [P, E])
        cnt = sb("cnt", [P, 4])
        gate = sb("gate", [P, E])
        hw = sb("hw", [P, ER])
        hwT = sb("hwT", [P, 2, P], F16)
        a_t = sb("a_t", [P, CHUNKS, H])
        tmp = sb("tmp", [P, CHUNKS, H])
        la = sb("la", [P, CHUNKS, H])
        part = sb("part", [P, PARTS, CHUNKS, H], BF16)
        rec = sb("rec", [P, 2 * STEPS, REC])
        zst = sb("zst", [P, GC])
        ps = [ctx.enter_context(nc.psum_tensor(f"p_ps{i}", [P, 512], F32)) for i in range(8)]
        PT, PA, PB, PH, PD = ps[0:2], ps[2], ps[3:5], ps[5], ps[6:8]

        s_cst = sem("cst")
        s_x = [sem("x0"), sem("x1")]
        s_w = [sem("w0"), sem("w1")]
        s_whi, s_wlo = sem("whi"), sem("wlo")
        s_init = sem("init")
        s_st, s_mv, s_ve, s_rs, s_xnr = sem("st"), sem("mv"), sem("ve"), sem("rs"), sem("xnr")
        s_tr, s_hi, s_lo = sem("tr"), sem("hi"), sem("lo")
        s_aux, s_auxs, s_sm, s_hw = sem("aux"), sem("auxs"), sem("sm"), sem("hw")
        s_ht, s_hh, s_hl = sem("ht"), sem("hh"), sem("hl")
        s_base, s_xb, s_or = sem("base"), sem("xb"), sem("or")
        s_o = [sem("o0"), sem("o1")]
        s_xd, s_z, s_rec = sem("xd"), sem("z"), sem("rec")
        s_dec, s_ddec, s_pdec = sem("dec"), sem("ddec"), sem("pdec")
        block = ctx.enter_context(nc.Block())
        NCST = 8

        @block.sync
        def _(sp):
            sp.dma_start(cst[:], ext["cst"]).then_inc(s_cst, 16)
            for i, t in enumerate(("dt_bias", "b_router", "A_log", "D", "b_base")):
                dst = (bias_row[:, 0:H], bias_row[:, H:H + E], alog[:], dvec[:], bbase[:])[i]
                sp.dma_start(dst, ext[t].to_broadcast([P, dst.shape[1]])).then_inc(s_cst, 16)
            sp.dma_start(nwall[:], ext["norm_w"]).then_inc(s_cst, 16)
            sp.dma_start(keep["cw"][:], ext["conv"]).then_inc(s_cst, 16)

            def x_row(i):
                if i >= 2:
                    sp.wait_ge(s_or, i - 1)
                sp.dma_start(xrow[:, i % 2, :], ext["x"][rows[i] * P:(rows[i] + 1) * P, :]).then_inc(s_x[i % 2], 16)

            x_row(0)
            x_row(1)
            srcs = [ext["w_base"][k] for k in range(KT)] + [ext["w_aux"][k] for k in range(2)] + [ext["lora_B"]]
            order = [KT, KT + 1] + list(range(KT)) + [KT + 2]
            for n, q in enumerate(order):
                if n >= 2:
                    sp.wait_ge(s_wlo, n - 1)
                sp.dma_start(stage[:, n % 2, 0:srcs[q].shape[1]], srcs[q]).then_inc(s_w[n % 2], 16)
            sp.wait_ge(s_init, 1)
            for g in range(G):
                sp.dma_start(d["state"][g], zst[:]).then_inc(s_z, 16)
            for i in range(CHUNKS):
                sp.wait_ge(s_or, i + 1)
                r = rows[i]
                sp.dma_start(d["part_out"][r * P:(r + 1) * P, :], orow[:, i % 2, :]).then_inc(s_o[i % 2], 16)
                if i + 2 < CHUNKS:
                    sp.dma_start(xrow[:, i % 2, :], ext["x"][rows[i + 2] * P:(rows[i + 2] + 1) * P, :]).then_inc(s_x[i % 2], 16)
                if i % NC == NC - 1 and i // NC < 2:
                    t = i // NC
                    sp.wait_ge(s_lo, 2 * (i + 1))
                    sp.dma_start(d["xn"][t], xn[:, t].rearrange("p k h t -> p (k h t)")).then_inc(s_xd, 16)
            sp.wait_ge(s_rec, 1)
            sp.dma_start(d["rec"], rec[:]).then_inc(s_dec, 16)
            sp.wait_ge(s_dec, 16)
            sp.wait_ge(s_z, 16 * G)
            sp.wait_ge(s_xd, 32)
            for b in range(2):
                sp.wait_ge(s_o[b], 16 * (CHUNKS // 2))

        order = [KT, KT + 1] + list(range(KT)) + [KT + 2]

        def wview(q, h):
            if q < KT:
                return Wb[:, q, h, :]
            if q < KT + 2:
                return Wb[:, q, h, 0:4 * AUX]
            return Wb[:, q, h, :]

        @block.scalar
        def _(act):
            act.wait_ge(s_cst, 16 * NCST)
            nc.scalar.activation(expa[:], alog[:], ACT.Exp).then_inc(s_pdec, 1)

            def split(n):
                q = order[n]
                act.wait_ge(s_w[n % 2], 16 * (n // 2 + 1))
                w = wview(q, 0)
                nc.scalar.activation(w, stage[:, n % 2, 0:w.shape[1]], ACT.Copy, scale=SCALE).then_inc(s_whi, 1)

            done = 0
            for i in range(CHUNKS):
                T, c = i // NC, i % NC
                for b in range(2):
                    act.wait_ge(s_tr, 2 * i + b + 1)
                    if c == 0 and T >= 2:
                        act.wait_ge(s_base, 2 * NC * (T - 1))
                        act.wait_ge(s_xd, 16 * (T - 1))
                    nc.scalar.activation(xn[:, T % 2, 4 * b:4 * b + 4, 0, c * P:(c + 1) * P],
                                         PT[b][:].rearrange("p (k t) -> p k t", k=4), ACT.Copy).then_inc(s_hi, 1)
                while done < min(NF, 4 * (i + 1)) or (i == 0 and done < NF):
                    split(done)
                    done += 1
                act.wait_ge(s_aux, i + 1)
                if i:
                    act.wait_ge(s_hw, i)
                nc.scalar.activation(aux[:], PA[:, 0:AUX], ACT.Copy, scale=1.0 / SCALE).then_inc(s_auxs, 1)
                act.wait_ge(s_ht, i + 1)
                if i:
                    act.wait_ge(s_base, 2 * i)
                nc.scalar.activation(hwT[:, 0, :], PH[:, 0:P], ACT.Copy).then_inc(s_hh, 1)
            act.wait_ge(s_ddec, 1)
            nc.scalar.activation(tmp[:], tmp[:], ACT.Exp).then_inc(s_pdec, 1)
            act.wait_ge(s_pdec, 2)
            nc.scalar.activation(tmp[:], tmp[:], ACT.Ln, bias=onesf[:, 0:1]).then_inc(s_pdec, 1)
            for n, arr in enumerate((A_ELA, A_W, A_ETOT)):
                for b in range(2):
                    act.wait_ge(s_tr, 2 * CHUNKS + 2 * n + b + 1)
                    for s in range(2):
                        o = arr * NC * HG
                        dst = rec[:, :, o:o + NC * HG].rearrange("p (f g s) (c h) -> p f s g c h", f=2, s=2, h=HG)
                        last = nc.scalar.activation(
                            dst[:, b, s], PD[b][:].rearrange("p (s c g h) -> p s g c h", s=2, c=NC, h=HG)[:, s], ACT.Exp)
                    last.then_inc(s_hi, 1)

        @block.gpsimd
        def _(pool):
            nc.gpsimd.memset(mhalf[:], LN_POW).then_inc(s_init, 1)
            pool.wait_ge(s_init, 4)
            for i in range(CHUNKS):
                pool.wait_ge(s_ve, i + 1)
                nc.gpsimd.tensor_tensor(rstd[:], veps[:], mhalf[:], ALU.pow).then_inc(s_rs, 1)

        @block.vector
        def _(dve):
            chain = [0]
            s_c = keep["s_chain"]

            def link(ins):
                chain[0] += 1
                ins.then_inc(s_c, 1)
                dve.wait_ge(s_c, chain[0])

            nc.vector.memset(zst[:], 0.0).then_inc(s_init, 1)
            nc.vector.memset(keep["halo"][:], 0.0).then_inc(s_init, 1)
            link(nc.vector.memset(onesf[:], 1.0))
            dve.wait_ge(s_cst, 16 * NCST)
            nc.vector.tensor_copy(ident32[:], cst[:, C_ID:C_ID + P])
            nc.vector.tensor_copy(keep["ident16"][:], cst[:, C_ID:C_ID + P])
            nc.vector.tensor_copy(keep["identb"][:], cst[:, C_ID:C_ID + P])
            for h in range(4):
                nc.vector.tensor_copy(keep["neg"][:, h, :], cst[:, C_NEG:C_NEG + P])
            link(nc.vector.tensor_copy(keep["hot"][:], cst[0:LAW, C_HOT:C_HOT + HG * P]))
            nc.vector.tensor_scalar(nwall[:], nwall[:], SCALE, None, ALU.mult).then_inc(s_init, 1)

            def split(n):
                q = order[n]
                dve.wait_ge(s_whi, n + 1)
                hi, lo = wview(q, 0), wview(q, 1)
                nc.vector.scalar_tensor_tensor(lo, stage[:, n % 2, 0:lo.shape[1]], SCALE, hi,
                                               op0=ALU.mult, op1=ALU.subtract).then_inc(s_wlo, 1)

            def norm(i):
                dve.wait_ge(s_x[i % 2], 16 * (i // 2 + 1))
                nc.vector.bn_stats(stats[:, 0, :], xrow[:, i % 2, 0:512])
                link(nc.vector.bn_stats(stats[:, 1, :], xrow[:, i % 2, 512:DM]))
                link(nc.vector.bn_aggr(mv[:], stats[:]))
                if i:
                    dve.wait_ge(s_rs, i)
                nc.vector.tensor_scalar(veps[:], mv[:, 1:2], EPS, None, ALU.add).then_inc(s_ve, 1)
                dve.wait_ge(s_rs, i + 1)
                if i:
                    dve.wait_ge(s_tr, 2 * i)
                nc.vector.tensor_scalar(xnrow[:], xrow[:, i % 2, :], mv[:, 0:1], rstd[:, 0:1],
                                        ALU.subtract, ALU.mult).then_inc(s_xnr, 1)

            def low(i):
                T, c = i // NC, i % NC
                for b in range(2):
                    dve.wait_ge(s_hi, 2 * i + b + 1)
                    hl = xn[:, T % 2, 4 * b:4 * b + 4, :, c * P:(c + 1) * P]
                    nc.vector.tensor_tensor(hl[:, :, 1, :], PT[b][:].rearrange("p (k t) -> p k t", k=4),
                                            hl[:, :, 0, :], ALU.subtract).then_inc(s_lo, 1)

            norm(0)
            low(0)
            for n in range(NF):
                split(n)
            for i in range(CHUNKS):
                if i + 1 < CHUNKS:
                    norm(i + 1)
                dve.wait_ge(s_auxs, i + 1)
                nc.vector.tensor_tensor(dtraw[:, rows[i], :], aux[:, 0:H], bias_row[:, 0:H], ALU.add)
                link(nc.vector.tensor_tensor(gate[:], aux[:, H:H + E], bias_row[:, H:H + E], ALU.add))
                link(nc.vector.max(zs[:], gate[:]))
                src = zs[:]
                for n, sh in enumerate((1, 2, 4)):
                    dst = cum[:, n % 2, :]
                    nc.vector.tensor_copy(dst[:, 0:sh], src[:, 0:sh])
                    link(nc.vector.tensor_tensor(dst[:, sh:E], src[:, sh:E], src[:, 0:E - sh], ALU.add))
                    src = dst
                link(nc.vector.tensor_tensor(kz[:], zs[:], cst[:, C_K:C_K + E], ALU.mult))
                link(nc.vector.scalar_tensor_tensor(sup[:], kz[:], 1.0, src, op0=ALU.add, op1=ALU.is_gt))
                link(nc.vector.tensor_reduce(cnt[:, 0:1], sup[:], AX.X, ALU.add))
                link(nc.vector.scalar_tensor_tensor(sup[:], cst[:, C_K:C_K + E], cnt[:, 0:1], src,
                                                    op0=ALU.is_equal, op1=ALU.mult))
                nc.vector.reciprocal(cnt[:, 1:2], cnt[:, 0:1])
                link(nc.vector.tensor_reduce(cnt[:, 2:3], sup[:], AX.X, ALU.add))
                link(nc.vector.tensor_scalar(cnt[:, 3:4], cnt[:, 2:3], -1.0, cnt[:, 1:2], ALU.add, ALU.mult))
                link(nc.vector.tensor_scalar(gate[:], gate[:], cnt[:, 3:4], 0.0, ALU.subtract, ALU.max))
                if i:
                    dve.wait_ge(s_ht, i)
                nc.vector.tensor_tensor(hw[:].rearrange("p (e r) -> p e r", r=R),
                                        aux[:, H + E:AUX].rearrange("p (e r) -> p e r", r=R),
                                        gate[:].unsqueeze(2).to_broadcast([P, E, R]), ALU.mult).then_inc(s_hw, 1)
                if i >= 2:
                    dve.wait_ge(s_o[i % 2], 16 * (i // 2))
                nc.vector.tensor_tensor(orow[:, i % 2, :], xrow[:, i % 2, :], bbase[:], ALU.add).then_inc(s_xb, 1)
                dve.wait_ge(s_hh, i + 1)
                nc.vector.tensor_tensor(hwT[:, 1, :], PH[:, 0:P], hwT[:, 0, :], ALU.subtract).then_inc(s_hl, 1)
                if i + 1 < CHUNKS:
                    low(i + 1)
                dve.wait_ge(s_xb, i + 1)
                for b in range(2):
                    dve.wait_ge(s_base, 2 * i + b + 1)
                    o = orow[:, i % 2, b * 512:(b + 1) * 512]
                    last = nc.vector.scalar_tensor_tensor(o, PB[b][:], 1.0 / SCALE, o, op0=ALU.mult, op1=ALU.add)
                last.then_inc(s_or, 1)
            nc.vector.scalar_tensor_tensor(tmp[:], dtraw[:], -1.0, dtraw[:], op0=ALU.mult, op1=ALU.min).then_inc(s_ddec, 1)
            dve.wait_ge(s_pdec, 3)
            link(nc.vector.scalar_tensor_tensor(dtraw[:], dtraw[:], 0.0, tmp[:], op0=ALU.max, op1=ALU.add))
            nc.vector.scalar_tensor_tensor(a_t[:], dtraw[:], -1.0, expa[:].unsqueeze(1).to_broadcast([P, CHUNKS, H]),
                                           op0=ALU.mult, op1=ALU.mult).then_inc(s_ddec, 1)

            def rec4(src, o, w, neg=None):
                dst = rec[:, :, o:o + NC * HG].rearrange("p (f g s) (c h) -> p f s g c h", f=2, s=2, h=HG)
                s4 = src.rearrange("p (f s c) (g h) -> p f s g c h", f=2, s=2, h=HG)
                for f in range(2):
                    for s in range(2):
                        nc.vector.tensor_scalar(dst[:, f, s], s4[:, f, s], w, None, ALU.mult)

            rec4(dtraw[:], A_DT * NC * HG, 1.0)
            recg = rec[:, :, REC_D:REC_D + HG].rearrange("p (f g s) h -> p f s g h", f=2, s=2)
            recn = rec[:, :, REC_NW:REC_NW + XT].rearrange("p (f g s) h -> p f s g h", f=2, s=2)
            for f in range(2):
                for s in range(2):
                    nc.vector.tensor_copy(recg[:, f, s], dvec[:].rearrange("p (g h) -> p g h", h=HG))
                    nc.vector.tensor_copy(recn[:, f, s], nwall[:].rearrange("p (g h) -> p g h", h=XT))
            for b in range(2):
                dve.wait_ge(s_hi, 2 * CHUNKS + b + 1)
                dve.wait_ge(s_tr, 2 * CHUNKS + b + 1)
                link(nc.vector.tensor_copy(la[:].rearrange("p c h -> p (c h)")[:, b * 512:(b + 1) * 512], PD[b][:]))
                nc.vector.tensor_scalar(la[:, 0, 0:1], la[:, 0, 0:1], 1.0, None, ALU.mult).then_inc(s_ddec, 1)
            dve.wait_ge(s_ddec, 4)
            rec4(la[:], A_NLA * NC * HG, -1.0)
            cur = la
            for n in range(PARTS):
                link(nc.vector.tensor_copy(part[:, n], cur[:]))
                if n + 1 < PARTS:
                    link(nc.vector.tensor_tensor(tmp[:], cur[:], part[:, n], ALU.subtract))
                    cur = tmp
            recb = rec[:].rearrange("p u w -> p (u w)").bitcast(BF16).rearrange("p (u w) -> p u w", w=2 * REC)
            recb = recb[:, :, 2 * REC_LA:2 * REC].rearrange("p (f g s) (c n h) -> p f s g c n h", f=2, s=2, n=PARTS, h=HG)
            for n in range(PARTS):
                s4 = part[:, n].rearrange("p (f s c) (g h) -> p f s g c h", f=2, s=2, h=HG)
                for f in range(2):
                    for s in range(2):
                        last = nc.vector.tensor_copy(recb[:, f, s, :, :, n, :], s4[:, f, s])
            link(last)
            dve.wait_ge(s_hi, 2 * CHUNKS + 6)
            nc.vector.tensor_copy(cnt[:, 0:1], cnt[:, 1:2]).then_inc(s_rec, 1)

        @block.tensor
        def _(pe):
            pe.wait_ge(s_init, 4)

            def transposes(i):
                for b in range(2):
                    pe.wait_ge(s_xnr, i + 1)
                    if i:
                        pe.wait_ge(s_lo, 2 * (i - 1) + b + 1)
                    for k in range(4):
                        last = nc.tensor.transpose(PT[b][:, k * P:(k + 1) * P], xnrow[:, (4 * b + k) * P:(4 * b + k + 1) * P], ident32[:])
                    last.then_inc(s_tr, 1)

            def three(out, lhs, rhs, first, stop):
                for n, (a, b) in enumerate(((0, 0), (0, 1), (1, 0))):
                    last = nc.tensor.matmul(out, lhs(a), rhs(b), start=first and n == 0, stop=stop and n == 2)
                return last

            transposes(0)
            for i in range(CHUNKS):
                T, c = i // NC, i % NC
                pe.wait_ge(s_lo, 2 * (i + 1))
                def xl(k):
                    return lambda h: xn[:, T % 2, k, h, c * P:(c + 1) * P]
                if i == 0:
                    pe.wait_ge(s_wlo, 2)
                else:
                    pe.wait_ge(s_auxs, i)
                for k in range(KT):
                    last = three(PA[:, 0:AUX], xl(k),
                                 lambda h: Wb[:, KT + k // 4, h, (k % 4) * AUX:(k % 4 + 1) * AUX], k == 0, k == KT - 1)
                last.then_inc(s_aux, 1)
                if i + 1 < CHUNKS:
                    transposes(i + 1)
                if i == 0:
                    pe.wait_ge(s_wlo, NF)
                else:
                    pe.wait_ge(s_or, i)
                for b in range(2):
                    for k in range(KT):
                        three(PB[b][:], xl(k), lambda h: Wb[:, k, h, b * 512:(b + 1) * 512], k == 0, False)
                    if b == 0:
                        pe.wait_ge(s_hw, i + 1)
                        if i:
                            pe.wait_ge(s_hl, i)
                        nc.tensor.transpose(PH[:, 0:P], hw[:], ident32[:]).then_inc(s_ht, 1)
                pe.wait_ge(s_hl, i + 1)
                for b in range(2):
                    three(PB[b][:], lambda h: hwT[:, h, :], lambda h: Wb[:, KT + 2, h, b * 512:(b + 1) * 512],
                          False, True).then_inc(s_base, 1)
            pe.wait_ge(s_ddec, 2)
            for n, mat in enumerate((cst[:, C_LE:C_LE + P], cst[:, C_GT:C_GT + P], onesf[:])):
                for b in range(2):
                    if n:
                        pe.wait_ge(s_hi, 2 * CHUNKS + 2 * (n - 1) + b + 1)
                    if n == 1:
                        pe.wait_ge(s_ddec, 3 + b)
                    nc.tensor.matmul(PD[b][:], mat, a_t[:].rearrange("p c h -> p (c h)")[:, b * 512:(b + 1) * 512],
                                     start=True, stop=True).then_inc(s_tr, 1)


OUT_SLOTS = [NU + n for n in range(XT)]
SPLITS = {(0, 0, 1): OUT_SLOTS[:2], (0, 1, 0): OUT_SLOTS[2:], (0, 1, 1): [0, 1], (0, 2, 1): [2, 3], (0, 3, 1): [4, 5],
          (1, 0, 1): [6, 7], (1, 1, 1): [8, 9]}
STREAM = [q for key in sorted(SPLITS) for q in SPLITS[key]]
NSTREAM = len(STREAM)
FILL = (1, 1, 1, 2)
HALVES = sum(FILL)


def units_done(c, place):
    first = c * HALVES + sum(FILL[:place])
    return [h // 2 for h in range(first, first + FILL[place]) if h % 2]


def main_loop(nc, ext, d, keep):
    xn, W, ident32, stage = keep["xn"], keep["W"], keep["ident32"], keep["stage"]
    ident16, identb, neg, hot, cw, halo = (keep[k] for k in ("ident16", "identb", "neg", "hot", "cw", "halo"))
    with ExitStack() as ctx:
        def sb(name, shape, dt=F32):
            return ctx.enter_context(nc.sbuf_tensor("m_" + name, shape, dt))

        def sem(name):
            return ctx.enter_context(nc.semaphore("m_" + name))

        acc = sb("acc", [P, 2, NC, DM])
        state_in = sb("state_in", [P, GC])
        state = sb("state", [P, GC])
        st16 = sb("st16", [P, 2, GC], F16)
        raw = sb("raw", [P, 2, TAPS - 1 + ST])
        conv = sb("conv", [P, 2, ST])
        xT = sb("xT", [P, 2, XT, ST])
        bc = sb("bc", [P, 2, 2, 2, ST], F16)
        sg = sb("sg", [P, NC, GC])
        xs = sb("xs", [P, GC])
        dtx = sb("dtx", [P, GC])
        dx16 = sb("dx16", [P, 2, GC], F16)
        wx16 = sb("wx16", [P, 2, GC], F16)
        dec = sb("dec", [P, HG, P])
        g16 = sb("g16", [P, 2, HG, P], F16)
        y = sb("y", [P, GC])
        z16 = sb("z16", [P, 2, GC], F16)
        squares = sb("squares", [P, GC], F16)
        zT16 = sb("zT16", [P, 2, XT, P], F16)
        bs16 = sb("bs16", [P, 2, P], F16)
        laT = sb("laT", [LAW, P], BF16)
        rec = sb("rec", [P, 2, REC])
        cwg = sb("cwg", [P, CW])
        tail = sb("tail", [P, NCT, TAPS - 1])
        sumsq = sb("sumsq", [P, 2])
        var = sb("var", [P, 2])
        rstd = sb("rstd", [P, 2])
        mhalf = sb("mhalf", [P, 1])
        ps = [ctx.enter_context(nc.psum_tensor(f"m_ps{i}", [P, 512], F32)) for i in range(8)]
        p_proj, p_out, p_x, p_misc, p_dec, p_y, p_v = ps[0:2], ps[2], ps[3], ps[4], ps[5], ps[6], ps[7]
        p_misc16 = p_misc[:].bitcast(F16)
        p_miscb = p_misc[:].bitcast(BF16)
        p_bs = p_misc16[:, 0:2 * P].rearrange("p (h n) -> p h n", h=2)
        p_la = p_miscb[0:LAW, 2 * P:3 * P]
        p_cb = p_misc[:, 2 * P:3 * P]
        p_zT = p_x[:].bitcast(F16).rearrange("p (h i t) -> p h i t", h=2, i=XT)

        stage_full = [sem("stage_full0"), sem("stage_full1")]
        rec_full = [sem("rec_full0"), sem("rec_full1")]
        acc_full = [sem("acc_full0"), sem("acc_full1")]
        acc_stored = [sem("acc_stored0"), sem("acc_stored1")]
        xn_full = [sem("xn_full0"), sem("xn_full1")]
        state_full, state_stored = sem("state_full"), sem("state_stored")
        proj_done, xtr_done, misc_done, dec_done, inter_done, snew_done, intra_done, ztr_done, out_done = (
            sem(n) for n in ("proj_done", "xtr_done", "misc_done", "dec_done", "inter_done", "snew_done",
                             "intra_done", "ztr_done", "out_done"))
        w_high, proj_evac, silu_done, bc_high, xs_ready, misc_evac, dx_high, exp_done, wx_high, g_high, sq_done, z_high, st_high = (
            sem(n) for n in ("w_high", "proj_evac", "silu_done", "bc_high", "xs_ready", "misc_evac", "dx_high",
                             "exp_done", "wx_high", "g_high", "sq_done", "z_high", "st_high"))
        w_split, cw_ready, halo_in, conv_step, conv_done, bc_split, dtx_done, dx_split, t_done, ydx_done, wx_split, g_done, g_split, st_scaled, st_done, st_split, y_done, z_done, var_done, z_split, zt_evac, acc_done = (
            sem(n) for n in ("w_split", "cw_ready", "halo_in", "conv_step", "conv_done", "bc_split", "dtx_done",
                             "dx_split", "t_done", "ydx_done", "wx_split", "g_done", "g_split", "st_scaled",
                             "st_done", "st_split", "y_done", "z_done", "var_done", "z_split", "zt_evac", "acc_done"))
        wx_done, skip_done, rstd_done, mhalf_ready = (sem(n) for n in ("wx_done", "skip_done", "rstd_done", "mhalf_ready"))
        block = ctx.enter_context(nc.Block())

        def record(s, n, c):
            o = (n * NC + c) * HG
            return rec[:, s, o:o + HG]

        def heads(ap):
            return ap.rearrange("p (h q) -> p h q", q=HD)

        def per_head(row):
            return row.unsqueeze(2).to_broadcast([P, HG, HD])

        def splits_before(j, q):
            return NU + j * NSTREAM + STREAM.index(q) + 1

        def steps(engine, body):
            body(0, False)
            with engine.Fori(1, STEPS - 1) as j:
                body(j, False)
            body(STEPS - 1, True)

        @block.sync
        def _(sp):
            def weights(n, src, ring):
                at_least(sp, w_split, n - 1)
                sp.dma_start(stage[:, ring, :], src).then_inc(stage_full[ring], 16)

            def record_in(s, j):
                if not (isinstance(j, int) and j == 0):
                    at_least(sp, z_split, 8 * j - NC * (1 - s))
                sp.dma_start(rec[:, s, :], d["rec"][:, bass.ds(2 * j + s, 1), :]).then_inc(rec_full[s], 16)

            def state_load(j, g):
                at_least(sp, st_done, 8 * (j - 1) + 1)
                sp.dma_start(state_in[:], d["state"][bass.ds(g, 1), :, :].rearrange("a p c -> p (a c)")).then_inc(state_full, 16)

            acc_view = d["part_out"].rearrange("(f s c p) n -> f s p c n", f=2, s=2, p=P)
            out_view = d["out"].rearrange("(f s c p) n -> f s p c n", f=2, s=2, p=P)
            for q in range(NU):
                weights(q, ext["w_proj"][0, q], q % 2)
            record_in(0, 0)
            state_load(0, 0)
            record_in(1, 0)
            for s in range(2):
                sp.dma_start(acc[:, s], acc_view[0, s]).then_inc(acc_full[s], 16)

            def stream(j, g, gnext, lo, hi):
                for b in range(lo, hi):
                    q = STREAM[b]
                    src = (ext["w_out"][bass.ds(g, 1), q - NU] if q >= NU else ext["w_proj"][bass.ds(gnext, 1), q])
                    weights(NU + j * NSTREAM + b, src.rearrange("a p n -> p (a n)"), b % 2)

            def step(j, f, g):
                gnext = 0 if isinstance(g, int) else g + 1
                ahead = not (isinstance(j, int) and j == STEPS - 1)
                stream(j, g, gnext, 0, XT)
                if ahead:
                    stream(j, g, gnext, XT, XT + NCT)
                    record_in(0, j + 1)
                    at_least(sp, st_done, 8 * j + 1)
                    if f == 1:
                        at_least(sp, state_stored, 16 * G)
                    sp.dma_start(state_in[:], d["state"][bass.ds(gnext, 1), :, :].rearrange("a p c -> p (a c)")).then_inc(state_full, 16)
                    stream(j, g, gnext, XT + NCT, NSTREAM)
                at_least(sp, st_done, 8 * (j + 1))
                sp.dma_start(d["state"][bass.ds(g, 1), :, :].rearrange("a p c -> p (a c)"), state[:]).then_inc(state_stored, 16)
                if ahead:
                    record_in(1, j + 1)

            for f in range(2):
                with sp.Fori(0, G - 1) as g:
                    step(g + f * G, f, g)
                j = f * G + G - 1
                if f == 0:
                    stream(j, G - 1, 0, 0, XT)
                    at_least(sp, proj_done, NU * (2 * j + 1))
                    sp.dma_start(xn[:, 0].rearrange("p k h t -> p (k h t)"), d["xn"][0]).then_inc(xn_full[0], 16)
                    stream(j, G - 1, 0, XT, XT + NCT)
                    record_in(0, j + 1)
                    at_least(sp, st_done, 8 * j + 1)
                    at_least(sp, state_stored, 16 * (j + 1 - G + 0) if j + 1 - G > 0 else 16)
                    sp.dma_start(state_in[:], d["state"][0]).then_inc(state_full, 16)
                    at_least(sp, proj_done, NU * (2 * j + 2))
                    sp.dma_start(xn[:, 1].rearrange("p k h t -> p (k h t)"), d["xn"][1]).then_inc(xn_full[1], 16)
                    stream(j, G - 1, 0, XT + NCT, NSTREAM)
                    at_least(sp, acc_done, 2 * (8 * j + NC))
                    sp.dma_start(out_view[0, 0], acc[:, 0]).then_inc(acc_stored[0], 16)
                    at_least(sp, acc_stored[0], 16)
                    sp.dma_start(acc[:, 0], acc_view[1, 0]).then_inc(acc_full[0], 16)
                    at_least(sp, st_done, 8 * (j + 1))
                    sp.dma_start(d["state"][G - 1], state[:]).then_inc(state_stored, 16)
                    record_in(1, j + 1)
                    at_least(sp, acc_done, 2 * (8 * j + 8))
                    sp.dma_start(out_view[0, 1], acc[:, 1]).then_inc(acc_stored[1], 16)
                    at_least(sp, acc_stored[1], 16)
                    sp.dma_start(acc[:, 1], acc_view[1, 1]).then_inc(acc_full[1], 16)
                else:
                    stream(j, G - 1, 0, 0, XT)
                    at_least(sp, st_done, 8 * (j + 1))
                    sp.dma_start(d["state"][G - 1], state[:]).then_inc(state_stored, 16)
                    for s in range(2):
                        at_least(sp, acc_done, 2 * (8 * j + NC * (s + 1)))
                        sp.dma_start(out_view[1, s], acc[:, s]).then_inc(acc_stored[s], 16)
            at_least(sp, state_stored, 16 * STEPS)
            for s in range(2):
                at_least(sp, acc_stored[s], 32)

        @block.scalar
        def _(act):
            def split_high(j, n, q, ring, count):
                act.wait_ge(stage_full[ring], 16 * count)
                if not (isinstance(j, int) and j < 0):
                    if q < NCT:
                        at_least(act, proj_done, NU * (2 * j + 1) + q + 1)
                    elif q < NU:
                        at_least(act, proj_done, NU * (2 * j + 2))
                    else:
                        at_least(act, out_done, 2 * 8 * j)
                w = W[:, q, 0, :]
                if q < NU:
                    nc.scalar.activation(w, stage[:, ring, :], ACT.Copy, scale=SCALE).then_inc(w_high, 1)
                else:
                    nw = rec[:, 0, REC_NW + q - NU:REC_NW + q - NU + 1]
                    nc.scalar.activation(w, stage[:, ring, :], ACT.Copy, scale=nw).then_inc(w_high, 1)

            def unit_out(v, q, k):
                act.wait_ge(proj_done, NU * v + q + 1)
                if q < NCT:
                    at_least(act, conv_done, NCT * v + q - 1)
                    nc.scalar.activation(raw[:, q % 2, TAPS - 1:], p_proj[q % 2][:], ACT.Copy,
                                         scale=1.0 / SCALE).then_inc(proj_evac, 1)
                else:
                    at_least(act, z_done, NC * (v - 1) + q - NCT + 1)
                    nc.scalar.activation(sg[:, q - NCT, :], p_proj[q % 2][:], ACT.Silu,
                                         scale=1.0 / SCALE).then_inc(proj_evac, 1)

            def silu(v, vp, q):
                act.wait_ge(conv_done, NCT * v + q + 1)
                if q < XT:
                    if q == 0:
                        at_least(act, xtr_done, NC * (v - 1))
                    nc.scalar.activation(xT[:, vp, q, :], conv[:, q % 2, :], ACT.Silu).then_inc(silu_done, 1)
                else:
                    nc.scalar.activation(conv[:, q % 2, :], conv[:, q % 2, :], ACT.Silu).then_inc(silu_done, 1)
                    act.wait_ge(silu_done, NCT * v + q + 1)
                    if q == XT:
                        at_least(act, inter_done, NC * (v - 1))
                        at_least(act, misc_done, NC * (v - 1))
                    nc.scalar.activation(bc[:, vp, q - XT, 0, :], conv[:, q % 2, :], ACT.Copy).then_inc(bc_high, 1)

            def state_high(k, src):
                at_least(act, inter_done, k)
                nc.scalar.activation(st16[:, 0, :], src, ACT.Copy).then_inc(st_high, 1)

            def weights_high(j, s, c, place, last):
                for q in SPLITS.get((s, c, place), []):
                    if q >= NU or not last:
                        b = STREAM.index(q)
                        split_high(j, NU + j * NSTREAM + b, q, b % 2, NU // 2 + j * (NSTREAM // 2) + b // 2 + 1)

            for q in range(2):
                split_high(-1, q, q, q % 2, q // 2 + 1)
            for q in range(NU):
                for n in (2 * q + 2, 2 * q + 3):
                    if n < NU:
                        split_high(-1, n, n, n % 2, n // 2 + 1)
                if q < NCT:
                    unit_out(0, q, 0)
                if 1 <= q <= NCT:
                    silu(0, 0, q - 1)
                if q >= NCT:
                    unit_out(0, q, 0)
            act.wait_ge(state_full, 16)
            state_high(0, state_in[:])

            def body(j, last):
                for s in range(2):
                    ahead = not (last and s == 1)
                    v = 2 * j + s
                    for c in range(NC):
                        k = 8 * j + NC * s + c
                        if c == 0:
                            act.wait_ge(rec_full[s], 16 * (j + 1))
                        act.wait_ge(xtr_done, k + 1)
                        at_least(act, z_split, k)
                        nc.scalar.activation(xs[:], p_x[:], ACT.Copy).then_inc(xs_ready, 1)
                        act.wait_ge(misc_done, k + 1)
                        at_least(act, snew_done, k)
                        nc.scalar.activation(bs16[:], p_bs, ACT.Copy)
                        at_least(act, dec_done, 2 * k)
                        nc.scalar.activation(laT[:], p_la, ACT.Copy).then_inc(misc_evac, 1)
                        act.wait_ge(dtx_done, k + 1)
                        at_least(act, intra_done, k)
                        nc.scalar.activation(dx16[:, 0, :], dtx[:], ACT.Copy).then_inc(dx_high, 1)
                        weights_high(j, s, c, 0, last)
                        if ahead and c == 2:
                            silu(v + 1, (s + 1) % 2, 3)
                        if ahead:
                            for q in units_done(c, 0):
                                unit_out(v + 1, q, k)
                        for b in range(2):
                            act.wait_ge(dec_done, 2 * k + b + 1)
                            if b == 0:
                                at_least(act, g_split, k)
                            for h in range(4):
                                i = 4 * b + h
                                e = nc.scalar.activation(dec[:, i, :], p_dec[:, h * P:(h + 1) * P], ACT.Exp,
                                                         bias=record(s, A_NLA, c)[:, i:i + 1])
                            e.then_inc(exp_done, 1)
                            if b == 0:
                                act.wait_ge(wx_done, k + 1)
                                at_least(act, snew_done, k)
                                nc.scalar.activation(wx16[:, 0, :], dtx[:], ACT.Copy).then_inc(wx_high, 1)
                                if ahead:
                                    for q in units_done(c, 1):
                                        unit_out(v + 1, q, k)
                        act.wait_ge(g_done, k + 1)
                        at_least(act, intra_done, k)
                        nc.scalar.activation(g16[:, 0], dec[:], ACT.Copy).then_inc(g_high, 1)
                        if ahead:
                            for q in {1: [1], 2: [4]}.get(c, []):
                                silu(v + 1, (s + 1) % 2, q)
                        if not (last and s == 1 and c == NC - 1):
                            act.wait_ge(st_done, k + 1)
                            if s == 1 and c == NC - 1:
                                act.wait_ge(state_full, 16 * (j + 2))
                                state_high(k + 1, state_in[:])
                            else:
                                state_high(k + 1, state[:])
                        for q in units_done(c, 2) if ahead else []:
                            unit_out(v + 1, q, k)
                        act.wait_ge(y_done, k + 1)
                        nc.scalar.activation(squares[:], y[:], ACT.Square, accum_out=sumsq[:, c % 2:c % 2 + 1]).then_inc(sq_done, 1)
                        act.wait_ge(z_done, k + 1)
                        at_least(act, ztr_done, k)
                        nc.scalar.activation(z16[:, 0, :], xs[:], ACT.Copy).then_inc(z_high, 1)
                        weights_high(j, s, c, 1, last)
                        if ahead:
                            for q in {0: [0], 1: [2]}.get(c, []):
                                silu(v + 1, (s + 1) % 2, q)
                            for q in units_done(c, 3):
                                unit_out(v + 1, q, k)
                            if c == 2:
                                silu(v + 1, (s + 1) % 2, 5)

            steps(act, body)

        @block.gpsimd
        def _(pool):
            nc.gpsimd.memset(mhalf[:], LN_POW).then_inc(mhalf_ready, 1)
            pool.wait_ge(mhalf_ready, 1)

            def body(j, last):
                for s in range(2):
                    for c in range(NC):
                        k = 8 * j + NC * s + c
                        if c == 0:
                            pool.wait_ge(rec_full[s], 16 * (j + 1))
                        pool.wait_ge(dx_split, k + 1)
                        nc.gpsimd.tensor_tensor(heads(dtx[:]), heads(dtx[:]), per_head(record(s, A_W, c)),
                                                ALU.mult).then_inc(wx_done, 1)
                        nc.gpsimd.tensor_tensor(heads(xs[:]), heads(xs[:]), per_head(rec[:, s, REC_D:REC_D + HG]),
                                                ALU.mult).then_inc(skip_done, 1)
                        pool.wait_ge(var_done, k + 1)
                        at_least(pool, acc_done, 2 * (k - 1))
                        nc.gpsimd.tensor_tensor(rstd[:, c % 2:c % 2 + 1], var[:, c % 2:c % 2 + 1], mhalf[:],
                                                ALU.pow).then_inc(rstd_done, 1)

            steps(pool, body)

        @block.vector
        def _(dve):
            def split_low(q, ring, n):
                dve.wait_ge(w_high, n + 1)
                sc = SCALE if q < NU else rec[:, 0, REC_NW + q - NU:REC_NW + q - NU + 1]
                nc.vector.scalar_tensor_tensor(W[:, q, 1, :], stage[:, ring, :], sc, W[:, q, 0, :],
                                               op0=ALU.mult, op1=ALU.subtract).then_inc(w_split, 1)

            def weights_low(j, s, c, place, last):
                for q in SPLITS.get((s, c, place), []):
                    if q >= NU or not last:
                        b = STREAM.index(q)
                        split_low(q, b % 2, NU + j * NSTREAM + b)

            def group_constants(j):
                at_least(dve, conv_done, 2 * NCT * j)
                g = j % G
                nc.vector.tensor_copy(cwg[:], cw[:, bass.ds(g * CW, CW)]).then_inc(cw_ready, 1)
                dve.wait_ge(cw_ready, j + 1)

            def convolve(j, s, q):
                v = 2 * j + s
                o = q * (TAPS + 1)
                n = TAPS - 1
                r = raw[:, q % 2, :]
                a = conv[:, q % 2, :]
                w = lambda t: cwg[:, o + t:o + t + 1]
                carried = halo[:, bass.ds((j % G) * NCT * n + q * n, n)]
                dve.wait_ge(proj_evac, NU * v + q + 1)
                at_least(dve, silu_done, NCT * v + q - 1)
                if q >= XT:
                    at_least(dve, bc_split, 2 * v)
                nc.vector.tensor_copy(r[:, 0:n], carried if s == 0 else tail[:, q, :]).then_inc(halo_in, 1)
                nc.vector.tensor_scalar(a, r[:, n:n + ST], w(n), w(TAPS), ALU.mult, ALU.add).then_inc(conv_step, 1)
                dve.wait_ge(halo_in, NCT * v + q + 1)
                for t in range(n - 1, -1, -1):
                    dve.wait_ge(conv_step, n * (NCT * v + q) + n - t)
                    last = nc.vector.scalar_tensor_tensor(a, r[:, t:t + ST], w(t), a, op0=ALU.mult, op1=ALU.add)
                    if t:
                        last.then_inc(conv_step, 1)
                nc.vector.tensor_copy(tail[:, q, :] if s == 0 else carried, r[:, ST:ST + n]).then_inc(conv_done, 1)

            def bc_low(v, vp, q):
                dve.wait_ge(bc_high, 2 * v + q - XT + 1)
                nc.vector.tensor_tensor(bc[:, vp, q - XT, 1, :], conv[:, q % 2, :], bc[:, vp, q - XT, 0, :],
                                        ALU.subtract).then_inc(bc_split, 1)

            def state_low(k, src):
                dve.wait_ge(st_high, k + 1)
                nc.vector.tensor_tensor(st16[:, 1, :], src, st16[:, 0, :], ALU.subtract).then_inc(st_split, 1)

            def zt_out(k):
                dve.wait_ge(ztr_done, k + 1)
                at_least(dve, out_done, 2 * k)
                nc.vector.tensor_copy(zT16[:], p_zT).then_inc(zt_evac, 1)

            def add_out(k, b, s, c):
                dve.wait_ge(out_done, 2 * k + b + 1)
                if b == 0:
                    dve.wait_ge(rstd_done, k + 1)
                o = acc[:, s, c, b * 512:(b + 1) * 512]
                nc.vector.scalar_tensor_tensor(o, p_out[:], rstd[:, c % 2:c % 2 + 1], o, op0=ALU.mult,
                                               op1=ALU.add).then_inc(acc_done, 1)

            group_constants(0)
            for q in range(2):
                split_low(q, q % 2, q)
            for q in range(NU):
                for n in (2 * q + 2, 2 * q + 3):
                    if n < NU:
                        split_low(n, n % 2, n)
                if q < NCT:
                    convolve(0, 0, q)
                if XT + 1 <= q <= XT + 2:
                    bc_low(0, 0, q - 1)
            state_low(0, state_in[:])

            def body(j, last):
                for s in range(2):
                    ahead = not (last and s == 1)
                    v = 2 * j + s
                    nj, ns = (j, 1) if s == 0 else (j + 1, 0)
                    for c in range(NC):
                        k = 8 * j + NC * s + c
                        first = isinstance(k, int) and k == 0
                        ps_, pc = ((s, c - 1) if c else (1 - s, NC - 1))
                        if c == 0:
                            dve.wait_ge(rec_full[s], 16 * (j + 1))
                            if s == 1 and ahead:
                                group_constants(j + 1)
                        dve.wait_ge(xs_ready, k + 1)
                        at_least(dve, wx_split, k)
                        nc.vector.tensor_tensor(heads(dtx[:]), heads(xs[:]), per_head(record(s, A_DT, c)),
                                                ALU.mult).then_inc(dtx_done, 1)
                        dve.wait_ge(dx_high, k + 1)
                        nc.vector.tensor_tensor(dx16[:, 1, :], dtx[:], dx16[:, 0, :], ALU.subtract).then_inc(dx_split, 1)
                        weights_low(j, s, c, 0, last)
                        dve.wait_ge(inter_done, k + 1)
                        at_least(dve, sq_done, k)
                        nc.vector.tensor_tensor(heads(y[:]), heads(p_v[:]), per_head(record(s, A_ELA, c)),
                                                ALU.mult).then_inc(t_done, 1)
                        if not first:
                            zt_out(k - 1)
                        dve.wait_ge(wx_high, k + 1)
                        nc.vector.tensor_tensor(wx16[:, 1, :], dtx[:], wx16[:, 0, :], ALU.subtract).then_inc(wx_split, 1)
                        dve.wait_ge(skip_done, k + 1)
                        dve.wait_ge(t_done, k + 1)
                        nc.vector.tensor_tensor(y[:], y[:], xs[:], ALU.add).then_inc(ydx_done, 1)
                        src = state_in if s == 0 and c == 0 else state
                        if s == 0 and c == 0:
                            at_least(dve, state_stored, 16 * j)
                        nc.vector.tensor_tensor(heads(state[:]), heads(src[:]), per_head(record(s, A_ETOT, c)),
                                                ALU.mult).then_inc(st_scaled, 1)
                        for q in units_done(c, 0) + units_done(c, 1) if ahead else []:
                            if q < NCT:
                                convolve(nj, ns, q)
                        dve.wait_ge(exp_done, 2 * k + 2)
                        nc.vector.tensor_tensor(dec[:], dec[:], p_cb.unsqueeze(1).to_broadcast([P, HG, P]),
                                                ALU.mult).then_inc(g_done, 1)
                        if not first:
                            if c == 1:
                                dve.wait_ge(acc_full[s], 16 * (j // G + 1))
                            add_out(k - 1, 0, ps_, pc)
                        dve.wait_ge(g_high, k + 1)
                        nc.vector.tensor_tensor(g16[:, 1], dec[:], g16[:, 0], ALU.subtract).then_inc(g_split, 1)
                        dve.wait_ge(snew_done, k + 1)
                        dve.wait_ge(st_scaled, k + 1)
                        nc.vector.tensor_tensor(state[:], state[:], p_v[:], ALU.add).then_inc(st_done, 1)
                        if not first:
                            add_out(k - 1, 1, ps_, pc)
                        if not (last and s == 1 and c == NC - 1):
                            dve.wait_ge(st_done, k + 1)
                            state_low(k + 1, state_in[:] if (s == 1 and c == NC - 1) else state[:])
                        for q in units_done(c, 2) if ahead else []:
                            if q < NCT:
                                convolve(nj, ns, q)
                        dve.wait_ge(intra_done, k + 1)
                        dve.wait_ge(ydx_done, k + 1)
                        nc.vector.tensor_tensor(y[:], y[:], p_y[:], ALU.add).then_inc(y_done, 1)
                        dve.wait_ge(y_done, k + 1)
                        nc.vector.scalar_tensor_tensor(xs[:], y[:], SCALE, sg[:, c, :], op0=ALU.mult,
                                                       op1=ALU.mult).then_inc(z_done, 1)
                        dve.wait_ge(sq_done, k + 1)
                        at_least(dve, rstd_done, k - 1)
                        nc.vector.tensor_scalar(var[:, c % 2:c % 2 + 1], sumsq[:, c % 2:c % 2 + 1], OUT_POW2 / GC,
                                                EPS * OUT_POW2, ALU.mult, ALU.add).then_inc(var_done, 1)
                        dve.wait_ge(z_high, k + 1)
                        nc.vector.tensor_tensor(z16[:, 1, :], xs[:], z16[:, 0, :], ALU.subtract).then_inc(z_split, 1)
                        weights_low(j, s, c, 1, last)
                        if ahead and c == 2:
                            bc_low(v + 1, (s + 1) % 2, XT)
                        for q in units_done(c, 3) if ahead else []:
                            if q < NCT:
                                convolve(nj, ns, q)
                        if ahead and c == 2:
                            bc_low(v + 1, (s + 1) % 2, XT + 1)

            steps(dve, body)
            zt_out(STEPS * 8 - 1)
            for b in range(2):
                add_out(STEPS * 8 - 1, b, 1, NC - 1)

        @block.tensor
        def _(pe):
            def three(out, lhs, rhs, first, stop):
                for n, (a, b) in enumerate(((0, 0), (0, 1), (1, 0))):
                    last = nc.tensor.matmul(out, lhs(a), rhs(b), start=first and n == 0, stop=stop and n == 2)
                return last

            def half_unit(v, vp, h, ready):
                q, part = h // 2, h % 2
                out = p_proj[q % 2][:]
                if part == 0:
                    at_least(pe, proj_evac, NU * v + q - 1)
                    at_least(pe, w_split, ready(min(q, NCT) if q < NCT else NU - 1))
                for k in range(4 * part, 4 * part + 4):
                    if q < NCT:
                        last = three(out, lambda x: W[:, q, x, k * P:(k + 1) * P], lambda x: xn[:, vp, k, x, :],
                                     k == 0, k == KT - 1)
                    else:
                        t = (q - NCT) * P
                        last = three(out, lambda x: xn[:, vp, k, x, t:t + P],
                                     lambda x: W[:, NCT + k // 2, x, (k % 2) * 512:(k % 2 + 1) * 512],
                                     k == 0, k == KT - 1)
                if part:
                    last.then_inc(proj_done, 1)

            def out_half(k, b):
                at_least(pe, acc_done, 2 * k + b)
                for i in range(XT):
                    last = three(p_out[:], lambda x: zT16[:, x, i, :],
                                 lambda x: W[:, NU + i, x, b * 512:(b + 1) * 512], i == 0, i == XT - 1)
                last.then_inc(out_done, 1)

            def gated_transposes(k):
                pe.wait_ge(z_split, k + 1)
                for x in range(2):
                    for i in range(XT):
                        last = nc.tensor.transpose(p_zT[:, x, i, :], z16[:, x, i * P:(i + 1) * P], ident16[:])
                last.then_inc(ztr_done, 1)

            for h in range(2 * NU):
                half_unit(0, 0, h, lambda q: q + 1)

            def body(j, last_step):
                for s in range(2):
                    ahead = not (last_step and s == 1)
                    v = 2 * j + s
                    ready = (lambda q: NU if isinstance(j, int) and j == 0 else splits_before(j - 1, q)) if s == 0 else (
                        lambda q: splits_before(j, q))
                    for c in range(NC):
                        k = 8 * j + NC * s + c
                        first = isinstance(k, int) and k == 0
                        t = slice(c * P, (c + 1) * P)

                        def fill(place):
                            if ahead:
                                h0 = c * HALVES + sum(FILL[:place])
                                for h in range(h0, h0 + FILL[place]):
                                    if h == 0:
                                        at_least(pe, xn_full[1 - s], 16 * ((j if s == 0 else j + 1) // G))
                                    half_unit(v + 1, 1 - s, h, ready)

                        if c == 0:
                            pe.wait_ge(silu_done, NCT * v + XT)
                        at_least(pe, zt_evac, k - 1)
                        for i in range(XT):
                            last = nc.tensor.transpose(p_x[:, i * P:(i + 1) * P], xT[:, s, i, t], ident32[:])
                        last.then_inc(xtr_done, 1)
                        if c == 0:
                            pe.wait_ge(bc_split, 2 * (v + 1))
                            pe.wait_ge(rec_full[s], 16 * (j + 1))
                        at_least(pe, g_done, k)
                        for x in range(2):
                            nc.tensor.transpose(p_bs[:, x, :], bc[:, s, 0, x, t], ident16[:])
                        rb = rec[:, s, REC_LA:REC].bitcast(BF16)
                        nc.tensor.transpose(p_la, rb[:, c * LAW:(c + 1) * LAW], identb[:])
                        three(p_cb, lambda x: bc[:, s, 0, x, t], lambda x: bc[:, s, 1, x, t], True, True).then_inc(misc_done, 1)
                        fill(0)

                        def decays(b):
                            nc.tensor.matmul(p_dec[:], identb[:], neg[:].rearrange("p h t -> p (h t)"), start=True, stop=False)
                            for h in range(4):
                                i = 4 * b + h
                                last = nc.tensor.matmul(p_dec[:, h * P:(h + 1) * P], hot[:, i * P:(i + 1) * P], laT[:],
                                                        start=False, stop=h == 3)
                            last.then_inc(dec_done, 1)

                        pe.wait_ge(misc_evac, k + 1)
                        at_least(pe, exp_done, 2 * k)
                        decays(0)
                        pe.wait_ge(st_split, k + 1)
                        at_least(pe, st_done, k)
                        three(p_v[:], lambda x: bc[:, s, 1, x, t], lambda x: st16[:, x, :], True, True).then_inc(inter_done, 1)
                        if not first:
                            pe.wait_ge(xs_ready, k + 1)
                            gated_transposes(k - 1)
                        fill(1)
                        pe.wait_ge(exp_done, 2 * k + 1)
                        decays(1)
                        if not first:
                            if s == 0 and c == 1:
                                pe.wait_ge(w_split, splits_before(j, NU + XT - 1))
                            pe.wait_ge(zt_evac, k)
                            out_half(k - 1, 0)
                        pe.wait_ge(t_done, k + 1)
                        pe.wait_ge(wx_split, k + 1)
                        three(p_v[:], lambda x: bs16[:, x, :], lambda x: wx16[:, x, :], True, True).then_inc(snew_done, 1)
                        fill(2)
                        if not first:
                            out_half(k - 1, 1)
                        pe.wait_ge(g_split, k + 1)
                        pe.wait_ge(dx_split, k + 1)
                        at_least(pe, y_done, k)
                        for h in range(HG):
                            o = slice(h * HD, (h + 1) * HD)
                            last = three(p_y[:, o], lambda x: g16[:, x, h, :], lambda x: dx16[:, x, o], True, True)
                        last.then_inc(intra_done, 1)
                        fill(3)

            steps(pe, body)
            gated_transposes(STEPS * 8 - 1)
            pe.wait_ge(zt_evac, STEPS * 8)
            for b in range(2):
                out_half(STEPS * 8 - 1, b)


def layer(nc, ext, out):
    d = {
        "xn": nc.dram_tensor("xn_scratch", [2, P, KT * 2 * ST], F16).ap(),
        "rec": nc.dram_tensor("rec_scratch", [P, 2 * STEPS, REC], F32).ap(),
        "state": nc.dram_tensor("state_scratch", [G, P, GC], F32).ap(),
        "part_out": nc.dram_tensor("part_scratch", [L, DM], F32).ap(),
        "out": out,
    }
    with ExitStack() as ctx:
        def sb(name, shape, dt=F32):
            return ctx.enter_context(nc.sbuf_tensor(name, shape, dt))

        keep = {
            "xn": sb("xn_hl", [P, 2, KT, 2, ST], F16),
            "W": sb("W_hl", [P, NU + XT, 2, DM], F16),
            "stage": sb("stage_w", [P, 2, DM]),
            "ident32": sb("ident32", [P, P]),
            "ident16": sb("ident16", [P, P], F16),
            "identb": sb("identb", [P, P], BF16),
            "neg": sb("neg", [P, 4, P], BF16),
            "hot": sb("hot", [LAW, HG * P], BF16),
            "cw": sb("cw", [P, G * CW]),
            "halo": sb("halo", [P, G * NCT * (TAPS - 1)]),
            "s_chain": ctx.enter_context(nc.semaphore("s_chain")),
        }
        prologue(nc, ext, d, keep)
        main_loop(nc, ext, d, keep)


def kernel(**inputs):
    import numpy as np
    import concourse.bacc as bacc
    from concourse.bass_utils import run_bass_kernel_spmd

    a = {k.removeprefix("L0_"): np.asarray(v) for k, v in inputs.items()}
    I = H * HD
    w = a["attn_in_proj_w"]

    def k_major(rows):
        return rows.T.reshape(KT, P, -1).transpose(1, 0, 2)

    proj, conv = [], []
    cw = np.concatenate([a["attn_conv_weight"], a["attn_conv_bias"][:, None]], 1)
    for g in range(G):
        chans = [g * GC + i * P for i in range(XT)] + [I + g * NS, I + G * NS + g * NS]
        proj += [k_major(w[I + o:I + o + P]).reshape(P, -1) for o in chans]
        gate = k_major(w[g * GC:(g + 1) * GC])
        proj += [gate[:, 2 * i:2 * i + 2].reshape(P, -1) for i in range(4)]
        conv += [cw[o:o + P] for o in chans]
    aux = np.concatenate([w[-H:], a["ffn_W_router"], a["ffn_lora_A"].transpose(0, 2, 1).reshape(ER, DM)], 0)
    aux = k_major(aux).reshape(P, 2, 4 * AUX).transpose(1, 0, 2)
    r = np.arange(P)
    cst = np.zeros((P, CST), np.float32)
    cst[:, C_ID:C_ID + P] = np.eye(P)
    cst[:, C_LE:C_LE + P] = r[:, None] <= r[None, :]
    cst[:, C_GT:C_GT + P] = r[:, None] > r[None, :]
    cst[:, C_NEG:C_NEG + P] = np.where(r[:, None] > r[None, :], -1e38, 0.0)
    for n in range(PARTS):
        for h in range(HG):
            cst[n * HG + h, C_HOT + h * P:C_HOT + (h + 1) * P] = 1
    cst[:, C_K:] = np.arange(1, E + 1)
    arrays = {
        "x": a["attn_hidden_states"].reshape(L, DM),
        "w_proj": np.stack(proj).reshape(G, NU, P, DM),
        "w_out": a["attn_out_proj_w"].T.reshape(G, XT, P, DM),
        "conv": np.stack(conv).reshape(G * NCT, P, TAPS + 1).transpose(1, 0, 2).reshape(P, G * CW),
        "norm_w": a["attn_norm_weight"].reshape(G * XT, P).T,
        "dt_bias": a["attn_dt_bias"][None], "A_log": a["attn_A_log"][None], "D": a["attn_D"][None],
        "w_base": a["ffn_W_base"].T.reshape(KT, P, DM), "w_aux": aux,
        "b_base": a["ffn_b_base"][None], "b_router": a["ffn_b_router"][None],
        "lora_B": a["ffn_lora_B"].reshape(ER, DM), "cst": cst,
    }
    arrays = {"in_" + k: np.ascontiguousarray(v) for k, v in arrays.items()}
    nc = bacc.Bacc("TRN2", target_bir_lowering=False, num_devices=1)
    ext = {k[3:]: nc.dram_tensor(k, v.shape, mybir.dt.from_np(v.dtype), kind="ExternalInput").ap() for k, v in arrays.items()}
    out = nc.dram_tensor("out_0", (L, DM), F32, kind="ExternalOutput").ap()
    layer(nc, ext, out)
    res = run_bass_kernel_spmd(nc, [arrays], core_ids=[0])
    return res.results[0]["out_0"].reshape(1, L, DM)
```

```python
from contextlib import ExitStack

import concourse.bass as bass
from concourse import mybir

F32 = mybir.dt.float32
F16 = mybir.dt.float16
BF16 = mybir.dt.bfloat16
I32 = mybir.dt.int32
ALU = mybir.AluOpType
ACT = mybir.ActivationFunctionType
AX = mybir.AxisListType

P = 128
L = 2048
DM = 1024
KT = DM // P
H, HD, NS, G = 64, 64, 128, 8
HG = H // G
GC = HG * HD
XT = GC // P
TAPS = 4
NCT = XT + 2
NU = NCT + 4
ST = 512
NC = ST // P
CHUNKS = L // P
HALF = L // 2
STEPS = 2 * G
E, R = 8, 16
ER = E * R
AUX = H + E + ER
EPS = 1e-5
SCALE = 64.0
LN_POW = -0.5
OUT_POW2 = SCALE ** 4
A_DT, A_W, A_ELA, A_ETOT, A_NLA = range(5)
REC_D = 5 * NC * HG
REC_NW = REC_D + HG
REC_LA = REC_NW + XT
PARTS = 3
LAW = 32
REC = REC_LA + NC * LAW // 2
C_ID, C_LE, C_GT, C_NEG, C_HOT, C_K = 0, P, 2 * P, 3 * P, 4 * P, 4 * P + HG * P
CST = C_K + E
CW = NCT * (TAPS + 1)


def at_least(engine, sem, value):
    if isinstance(value, int) and value <= 0:
        return
    engine.wait_ge(sem, value)


def prologue(nc, ext, d, keep):
    xn, Wb, ident32, stage = keep["xn"], keep["W"], keep["ident32"], keep["stage"]
    ORDER = [2, 3, 0, 1]
    rows = [T * NC + c for T in ORDER for c in range(NC)]
    NF = KT + 3
    ring = lambda n: (n + SHIFT - NF) % RING
    order = [KT, KT + 1] + list(range(KT)) + [KT + 2]
    FIRST_SLOTS = NU + XT - NF
    TAKE, LOAD = 5, 3
    with ExitStack() as ctx:
        def sb(name, shape, dt=F32):
            return ctx.enter_context(nc.sbuf_tensor("p_" + name, shape, dt))

        def sem(name):
            return ctx.enter_context(nc.semaphore("p_" + name))

        xrow = sb("xrow", [P, 3, DM])
        xnrow = sb("xnrow", [P, 2, DM])
        orow = sb("orow", [P, 2, DM])
        bbase = sb("bbase", [P, DM])
        bias_row = sb("bias_row", [P, H + E])
        alog = sb("alog", [P, H])
        expa = sb("expa", [P, H])
        dvec = sb("dvec", [P, H])
        nwall = sb("nwall", [P, G * XT])
        cst = sb("cst", [P, CST])
        onesf = sb("onesf", [P, P])
        stats = sb("stats", [P, 2, 6])
        mv = sb("mv", [P, 2])
        veps = sb("veps", [P, 1])
        rstd = sb("rstd", [P, 1])
        mhalf = sb("mhalf", [P, 1])
        aux = sb("aux", [P, AUX])
        dtraw = sb("dtraw", [P, CHUNKS, H])
        zs = sb("zs", [P, E])
        cum = sb("cum", [P, 2, E])
        kz = sb("kz", [P, E])
        sup = sb("sup", [P, E])
        cnt = sb("cnt", [P, 4])
        gate = sb("gate", [P, E])
        hw = sb("hw", [P, ER])
        hwT = sb("hwT", [P, 2, P], F16)
        a_t = sb("a_t", [P, CHUNKS, H])
        tmp = sb("tmp", [P, CHUNKS, H])
        la = sb("la", [P, CHUNKS, H])
        part = sb("part", [P, PARTS, CHUNKS, H], BF16)
        rec = sb("rec", [P, 2 * STEPS, REC])
        zst = sb("zst", [P, GC])
        ps = [ctx.enter_context(nc.psum_tensor(f"p_ps{i}", [P, 512], F32)) for i in range(8)]
        PT, PA, PB, PH, PD = ps[0:2], ps[2], ps[3:5], ps[5], ps[6:8]

        s_cst = sem("cst")
        s_x = [sem("x0"), sem("x1"), sem("x2")]
        s_w = [sem(f"w{r}") for r in range(RING)]
        s_whi, s_wlo = sem("whi"), sem("wlo")
        s_init, s_mh = sem("init"), sem("mh")
        s_st, s_mv, s_ve, s_rs, s_xnr = sem("st"), sem("mv"), sem("ve"), sem("rs"), sem("xnr")
        s_tr, s_hi, s_lo = sem("tr"), sem("hi"), sem("lo")
        s_aux, s_auxs, s_sm, s_hw = sem("aux"), sem("auxs"), sem("sm"), sem("hw")
        s_ht, s_hh, s_hl = sem("ht"), sem("hh"), sem("hl")
        s_base, s_xb, s_or = sem("base"), sem("xb"), sem("or")
        s_o = [sem("o0"), sem("o1")]
        s_xd, s_z, s_rec = sem("xd"), sem("z"), sem("rec")
        s_dec, s_ddec, s_pdec = sem("dec"), sem("ddec"), sem("pdec")
        block = ctx.enter_context(nc.Block())
        NCST = 8

        @block.sync
        def _(sp):
            def x_row(i):
                sp.dma_start(xrow[:, i % 3, :], ext["x"][rows[i] * P:(rows[i] + 1) * P, :]).then_inc(s_x[i % 3], 16)

            x_row(0)
            sp.dma_start(cst[:], ext["cst"]).then_inc(s_cst, 16)
            for i, t in enumerate(("dt_bias", "b_router", "A_log", "D", "b_base")):
                dst = (bias_row[:, 0:H], bias_row[:, H:H + E], alog[:], dvec[:], bbase[:])[i]
                sp.dma_start(dst, ext[t].to_broadcast([P, dst.shape[1]])).then_inc(s_cst, 16)
            sp.dma_start(nwall[:], ext["norm_w"]).then_inc(s_cst, 16)
            sp.dma_start(keep["cw"][:], ext["conv"]).then_inc(s_cst, 16)

            x_row(1)
            srcs = [ext["w_base"][k] for k in range(KT)] + [ext["w_aux"][k] for k in range(2)] + [ext["lora_B"]]
            for n, q in enumerate(order):
                if n >= RING:
                    sp.wait_ge(s_wlo, n - RING + 1)
                sp.dma_start(stage[:, ring(n), 0:srcs[q].shape[1]], srcs[q]).then_inc(s_w[ring(n)], 16)
            x_row(2)
            sp.wait_ge(s_init, 1)
            for g in range(G):
                sp.dma_start(d["state"][g], zst[:]).then_inc(s_z, 16)
            for i in range(CHUNKS):
                sp.wait_ge(s_or, i + 1)
                r = rows[i]
                sp.dma_start(d["part_out"][r * P:(r + 1) * P, :], orow[:, i % 2, :]).then_inc(s_o[i % 2], 16)
                if i + 3 < CHUNKS:
                    x_row(i + 3)
                if i in (LOAD, TAKE + 1):
                    for q in range(RING) if i == LOAD else range(RING, 2 * RING):
                        if i == LOAD:
                            sp.wait_ge(s_wlo, NF)
                        else:
                            sp.wait_ge(keep["w_split"], q - RING + 1)
                        b = (q + SHIFT) % RING
                        sp.dma_start(stage[:, b, :], ext["w_proj"][0, q]).then_inc(keep["stage_full"][b], 16)
                if i % NC == NC - 1 and i // NC < 2:
                    t = i // NC
                    sp.wait_ge(s_lo, 2 * (i + 1))
                    sp.dma_start(d["xn"][t], xn[:, t].rearrange("p k h t -> p (k h t)")).then_inc(s_xd, 16)
            sp.wait_ge(s_rec, 1)
            sp.dma_start(d["rec"], rec[:]).then_inc(s_dec, 16)
            sp.wait_ge(s_dec, 16)
            sp.wait_ge(s_z, 16 * G)
            sp.wait_ge(s_xd, 32)
            for b in range(RING):
                sp.wait_ge(keep["stage_full"][b], 32)
            for b in range(2):
                sp.wait_ge(s_o[b], 16 * (CHUNKS // 2))

        def wview(q, h):
            return Wb[:, FIRST_SLOTS + q, h, 0:4 * AUX if KT <= q < KT + 2 else DM]

        @block.scalar
        def _(act):
            act.wait_ge(s_cst, 16 * NCST)
            nc.scalar.activation(expa[:], alog[:], ACT.Exp).then_inc(s_pdec, 1)

            def split(n):
                q = order[n]
                act.wait_ge(s_w[ring(n)], 16 * (n // RING + 1))
                w = wview(q, 0)
                nc.scalar.activation(w, stage[:, ring(n), 0:w.shape[1]], ACT.Copy, scale=SCALE).then_inc(s_whi, 1)

            for i in range(CHUNKS):
                T, c = i // NC, i % NC
                for b in range(2):
                    act.wait_ge(s_tr, 2 * i + b + 1)
                    if c == 0 and T >= 2:
                        act.wait_ge(s_base, 2 * NC * (T - 1))
                        act.wait_ge(s_xd, 16 * (T - 1))
                    nc.scalar.activation(xn[:, T % 2, 4 * b:4 * b + 4, 0, c * P:(c + 1) * P],
                                         PT[b][:].rearrange("p (k t) -> p k t", k=4), ACT.Copy).then_inc(s_hi, 1)
                if i == 0:
                    split(0)
                    split(1)
                act.wait_ge(s_aux, i + 1)
                if i:
                    act.wait_ge(s_hw, i)
                nc.scalar.activation(aux[:], PA[:, 0:AUX], ACT.Copy, scale=1.0 / SCALE).then_inc(s_auxs, 1)
                if i == 0:
                    for n in range(2, NF):
                        split(n)
                if i == TAKE:
                    for q in range(FIRST_SLOTS):
                        b = (q + SHIFT) % RING
                        act.wait_ge(keep["stage_full"][b], 16)
                        nc.scalar.activation(Wb[:, q, 0, :], stage[:, b, :], ACT.Copy, scale=SCALE).then_inc(keep["w_high"], 1)
                act.wait_ge(s_ht, i + 1)
                if i:
                    act.wait_ge(s_base, 2 * i)
                nc.scalar.activation(hwT[:, 0, :], PH[:, 0:P], ACT.Copy).then_inc(s_hh, 1)
            act.wait_ge(s_ddec, 1)
            nc.scalar.activation(tmp[:], tmp[:], ACT.Exp).then_inc(s_pdec, 1)
            act.wait_ge(s_pdec, 2)
            nc.scalar.activation(tmp[:], tmp[:], ACT.Ln, bias=onesf[:, 0:1]).then_inc(s_pdec, 1)
            for n, arr in enumerate((A_ELA, A_W, A_ETOT)):
                for b in range(2):
                    act.wait_ge(s_tr, 2 * CHUNKS + 2 * n + b + 1)
                    for s in range(2):
                        o = arr * NC * HG
                        dst = rec[:, :, o:o + NC * HG].rearrange("p (f g s) (c h) -> p f s g c h", f=2, s=2, h=HG)
                        last = nc.scalar.activation(
                            dst[:, b, s], PD[b][:].rearrange("p (s c g h) -> p s g c h", s=2, c=NC, h=HG)[:, s], ACT.Exp)
                    last.then_inc(s_hi, 1)

        @block.gpsimd
        def _(pool):
            nc.gpsimd.memset(mhalf[:], LN_POW).then_inc(s_mh, 1)
            pool.wait_ge(s_mh, 1)
            for i in range(CHUNKS):
                pool.wait_ge(s_ve, i + 1)
                nc.gpsimd.tensor_tensor(rstd[:], veps[:], mhalf[:], ALU.pow).then_inc(s_rs, 1)

        @block.vector
        def _(dve):
            chain = [0]
            s_c = keep["s_chain"]

            def link(ins):
                chain[0] += 1
                ins.then_inc(s_c, 1)
                dve.wait_ge(s_c, chain[0])

            nc.vector.memset(zst[:], 0.0).then_inc(s_init, 1)
            nc.vector.memset(keep["halo"][:], 0.0).then_inc(s_init, 1)
            link(nc.vector.memset(onesf[:], 1.0))

            def norm(i):
                dve.wait_ge(s_x[i % 3], 16 * (i // 3 + 1))
                nc.vector.bn_stats(stats[:, 0, :], xrow[:, i % 3, 0:512])
                link(nc.vector.bn_stats(stats[:, 1, :], xrow[:, i % 3, 512:DM]))
                link(nc.vector.bn_aggr(mv[:], stats[:]))
                if i:
                    dve.wait_ge(s_rs, i)
                nc.vector.tensor_scalar(veps[:], mv[:, 1:2], EPS, None, ALU.add).then_inc(s_ve, 1)
                dve.wait_ge(s_rs, i + 1)
                if i >= 2:
                    dve.wait_ge(s_tr, 2 * (i - 1))
                nc.vector.tensor_scalar(xnrow[:, i % 2, :], xrow[:, i % 3, :], mv[:, 0:1], rstd[:, 0:1],
                                        ALU.subtract, ALU.mult).then_inc(s_xnr, 1)

            norm(0)
            dve.wait_ge(s_cst, 16 * NCST)
            nc.vector.tensor_copy(ident32[:], cst[:, C_ID:C_ID + P])
            nc.vector.tensor_copy(keep["ident16"][:], cst[:, C_ID:C_ID + P])
            nc.vector.tensor_copy(keep["identb"][:], cst[:, C_ID:C_ID + P])
            nc.vector.tensor_copy(keep["neg"][:], cst[:, C_NEG:C_NEG + P])
            nc.vector.memset(rec[:, :, REC_LA:REC], 0.0)
            link(nc.vector.tensor_copy(keep["hot"][:], cst[:, C_HOT:C_HOT + HG * P]))
            nc.vector.tensor_scalar(nwall[:], nwall[:], SCALE, None, ALU.mult).then_inc(s_init, 1)

            def split(n):
                q = order[n]
                dve.wait_ge(s_whi, n + 1)
                hi, lo = wview(q, 0), wview(q, 1)
                nc.vector.scalar_tensor_tensor(lo, stage[:, ring(n), 0:lo.shape[1]], SCALE, hi,
                                               op0=ALU.mult, op1=ALU.subtract).then_inc(s_wlo, 1)

            def low(i):
                T, c = i // NC, i % NC
                for b in range(2):
                    dve.wait_ge(s_hi, 2 * i + b + 1)
                    hl = xn[:, T % 2, 4 * b:4 * b + 4, :, c * P:(c + 1) * P]
                    nc.vector.tensor_tensor(hl[:, :, 1, :], PT[b][:].rearrange("p (k t) -> p k t", k=4),
                                            hl[:, :, 0, :], ALU.subtract).then_inc(s_lo, 1)

            norm(1)
            low(0)
            split(0)
            split(1)
            for i in range(CHUNKS):
                dve.wait_ge(s_auxs, i + 1)
                nc.vector.tensor_tensor(dtraw[:, rows[i], :], aux[:, 0:H], bias_row[:, 0:H], ALU.add)
                link(nc.vector.tensor_tensor(gate[:], aux[:, H:H + E], bias_row[:, H:H + E], ALU.add))
                link(nc.vector.max(zs[:], gate[:]))
                src = zs[:]
                for n, sh in enumerate((1, 2, 4)):
                    dst = cum[:, n % 2, :]
                    nc.vector.tensor_copy(dst[:, 0:sh], src[:, 0:sh])
                    link(nc.vector.tensor_tensor(dst[:, sh:E], src[:, sh:E], src[:, 0:E - sh], ALU.add))
                    src = dst
                link(nc.vector.tensor_tensor(kz[:], zs[:], cst[:, C_K:C_K + E], ALU.mult))
                link(nc.vector.scalar_tensor_tensor(sup[:], kz[:], 1.0, src, op0=ALU.add, op1=ALU.is_gt))
                link(nc.vector.tensor_reduce(cnt[:, 0:1], sup[:], AX.X, ALU.add))
                link(nc.vector.scalar_tensor_tensor(sup[:], cst[:, C_K:C_K + E], cnt[:, 0:1], src,
                                                    op0=ALU.is_equal, op1=ALU.mult))
                nc.vector.reciprocal(cnt[:, 1:2], cnt[:, 0:1])
                link(nc.vector.tensor_reduce(cnt[:, 2:3], sup[:], AX.X, ALU.add))
                link(nc.vector.tensor_scalar(cnt[:, 3:4], cnt[:, 2:3], -1.0, cnt[:, 1:2], ALU.add, ALU.mult))
                link(nc.vector.tensor_scalar(gate[:], gate[:], cnt[:, 3:4], 0.0, ALU.subtract, ALU.max))
                if i:
                    dve.wait_ge(s_ht, i)
                nc.vector.tensor_tensor(hw[:].rearrange("p (e r) -> p e r", r=R),
                                        aux[:, H + E:AUX].rearrange("p (e r) -> p e r", r=R),
                                        gate[:].unsqueeze(2).to_broadcast([P, E, R]), ALU.mult).then_inc(s_hw, 1)
                if i >= 2:
                    dve.wait_ge(s_o[i % 2], 16 * (i // 2))
                nc.vector.tensor_tensor(orow[:, i % 2, :], xrow[:, i % 3, :], bbase[:], ALU.add).then_inc(s_xb, 1)
                if i == 0:
                    for n in range(2, NF):
                        split(n)
                dve.wait_ge(s_hh, i + 1)
                nc.vector.tensor_tensor(hwT[:, 1, :], PH[:, 0:P], hwT[:, 0, :], ALU.subtract).then_inc(s_hl, 1)
                if i + 1 < CHUNKS:
                    low(i + 1)
                if i + 2 < CHUNKS:
                    norm(i + 2)
                if i == TAKE:
                    for q in range(FIRST_SLOTS):
                        dve.wait_ge(keep["w_high"], q + 1)
                        nc.vector.scalar_tensor_tensor(Wb[:, q, 1, :], stage[:, (q + SHIFT) % RING, :], SCALE, Wb[:, q, 0, :],
                                                       op0=ALU.mult, op1=ALU.subtract).then_inc(keep["w_split"], 1)
                dve.wait_ge(s_xb, i + 1)
                for b in range(2):
                    dve.wait_ge(s_base, 2 * i + b + 1)
                    o = orow[:, i % 2, b * 512:(b + 1) * 512]
                    last = nc.vector.scalar_tensor_tensor(o, PB[b][:], 1.0 / SCALE, o, op0=ALU.mult, op1=ALU.add)
                last.then_inc(s_or, 1)
            nc.vector.scalar_tensor_tensor(tmp[:], dtraw[:], -1.0, dtraw[:], op0=ALU.mult, op1=ALU.min).then_inc(s_ddec, 1)
            dve.wait_ge(s_pdec, 3)
            link(nc.vector.scalar_tensor_tensor(dtraw[:], dtraw[:], 0.0, tmp[:], op0=ALU.max, op1=ALU.add))
            nc.vector.scalar_tensor_tensor(a_t[:], dtraw[:], -1.0, expa[:].unsqueeze(1).to_broadcast([P, CHUNKS, H]),
                                           op0=ALU.mult, op1=ALU.mult).then_inc(s_ddec, 1)

            def rec4(src, o, w):
                dst = rec[:, :, o:o + NC * HG].rearrange("p (f g s) (c h) -> p f s g c h", f=2, s=2, h=HG)
                s4 = src.rearrange("p (f s c) (g h) -> p f s g c h", f=2, s=2, h=HG)
                for f in range(2):
                    for s in range(2):
                        nc.vector.tensor_scalar(dst[:, f, s], s4[:, f, s], w, None, ALU.mult)

            rec4(dtraw[:], A_DT * NC * HG, 1.0)
            recg = rec[:, :, REC_D:REC_D + HG].rearrange("p (f g s) h -> p f s g h", f=2, s=2)
            recn = rec[:, :, REC_NW:REC_NW + XT].rearrange("p (f g s) h -> p f s g h", f=2, s=2)
            for f in range(2):
                for s in range(2):
                    nc.vector.tensor_copy(recg[:, f, s], dvec[:].rearrange("p (g h) -> p g h", h=HG))
                    nc.vector.tensor_copy(recn[:, f, s], nwall[:].rearrange("p (g h) -> p g h", h=XT))
            for b in range(2):
                dve.wait_ge(s_hi, 2 * CHUNKS + b + 1)
                dve.wait_ge(s_tr, 2 * CHUNKS + b + 1)
                link(nc.vector.tensor_copy(la[:].rearrange("p c h -> p (c h)")[:, b * 512:(b + 1) * 512], PD[b][:]))
                nc.vector.tensor_scalar(la[:, 0, 0:1], la[:, 0, 0:1], 1.0, None, ALU.mult).then_inc(s_ddec, 1)
            dve.wait_ge(s_ddec, 4)
            rec4(la[:], A_NLA * NC * HG, -1.0)
            cur = la
            for n in range(PARTS):
                link(nc.vector.tensor_copy(part[:, n], cur[:]))
                if n + 1 < PARTS:
                    link(nc.vector.tensor_tensor(tmp[:], cur[:], part[:, n], ALU.subtract))
                    cur = tmp
            recb = rec[:].rearrange("p u w -> p (u w)").bitcast(BF16).rearrange("p (u w) -> p u w", w=2 * REC)
            recb = recb[:, :, 2 * REC_LA:2 * REC].rearrange("p (f g s) (c n h) -> p f s g c n h", f=2, s=2, n=LAW // HG, h=HG)
            for n in range(PARTS):
                s4 = part[:, n].rearrange("p (f s c) (g h) -> p f s g c h", f=2, s=2, h=HG)
                for f in range(2):
                    for s in range(2):
                        last = nc.vector.tensor_copy(recb[:, f, s, :, :, n, :], s4[:, f, s])
            link(last)
            dve.wait_ge(s_hi, 2 * CHUNKS + 6)
            nc.vector.tensor_copy(cnt[:, 0:1], cnt[:, 1:2]).then_inc(s_rec, 1)

        @block.tensor
        def _(pe):
            pe.wait_ge(s_init, 3)

            def transposes(i):
                for b in range(2):
                    pe.wait_ge(s_xnr, i + 1)
                    if i:
                        pe.wait_ge(s_lo, 2 * (i - 1) + b + 1)
                    for k in range(4):
                        last = nc.tensor.transpose(PT[b][:, k * P:(k + 1) * P], xnrow[:, i % 2, (4 * b + k) * P:(4 * b + k + 1) * P], ident32[:])
                    last.then_inc(s_tr, 1)

            def three(out, lhs, rhs, first, stop):
                for n, (a, b) in enumerate(((0, 0), (0, 1), (1, 0))):
                    last = nc.tensor.matmul(out, lhs(a), rhs(b), start=first and n == 0, stop=stop and n == 2)
                return last

            transposes(0)
            for i in range(CHUNKS):
                T, c = i // NC, i % NC
                pe.wait_ge(s_lo, 2 * (i + 1))
                def xl(k):
                    return lambda h: xn[:, T % 2, k, h, c * P:(c + 1) * P]
                if i == 0:
                    pe.wait_ge(s_wlo, 2)
                else:
                    pe.wait_ge(s_auxs, i)
                for k in range(KT):
                    last = three(PA[:, 0:AUX], xl(k),
                                 lambda h: Wb[:, FIRST_SLOTS + KT + k // 4, h, (k % 4) * AUX:(k % 4 + 1) * AUX], k == 0, k == KT - 1)
                last.then_inc(s_aux, 1)
                if i + 1 < CHUNKS:
                    transposes(i + 1)
                if i:
                    pe.wait_ge(s_or, i)
                for b in range(2):
                    for k in range(KT):
                        if i == 0 and b == 0:
                            pe.wait_ge(s_wlo, 3 + k)
                        three(PB[b][:], xl(k), lambda h: Wb[:, FIRST_SLOTS + k, h, b * 512:(b + 1) * 512], k == 0, False)
                    if b == 0:
                        pe.wait_ge(s_hw, i + 1)
                        if i:
                            pe.wait_ge(s_hl, i)
                        nc.tensor.transpose(PH[:, 0:P], hw[:], ident32[:]).then_inc(s_ht, 1)
                pe.wait_ge(s_hl, i + 1)
                if i == 0:
                    pe.wait_ge(s_wlo, NF)
                for b in range(2):
                    three(PB[b][:], lambda h: hwT[:, h, :], lambda h: Wb[:, FIRST_SLOTS + KT + 2, h, b * 512:(b + 1) * 512],
                          False, True).then_inc(s_base, 1)
            pe.wait_ge(s_ddec, 2)
            for n, mat in enumerate((cst[:, C_LE:C_LE + P], cst[:, C_GT:C_GT + P], onesf[:])):
                for b in range(2):
                    if n:
                        pe.wait_ge(s_hi, 2 * CHUNKS + 2 * (n - 1) + b + 1)
                    if n == 1:
                        pe.wait_ge(s_ddec, 3 + b)
                    nc.tensor.matmul(PD[b][:], mat, a_t[:].rearrange("p c h -> p (c h)")[:, b * 512:(b + 1) * 512],
                                     start=True, stop=True).then_inc(s_tr, 1)


OUT_SLOTS = [NU + n for n in range(XT)]
SPLITS = {(0, 0, 1): OUT_SLOTS[:2], (0, 1, 0): OUT_SLOTS[2:], (0, 2, 1): [0, 1], (0, 3, 0): [2, 3],
          (0, 3, 1): [4], (1, 0, 0): [5], (1, 0, 1): [6, 7], (1, 1, 0): [8], (1, 1, 1): [9]}
SILU_MID, SILU_END = {1: [0, 1], 2: [2, 3], 3: [5, 6, 7]}, {2: [4]}
STREAM = [q for key in sorted(SPLITS) for q in SPLITS[key]]
NSTREAM = len(STREAM)
RING = 3
SHIFT = (NSTREAM - NU) % RING
FIRST_USES = [sum((q + SHIFT) % RING == r for q in range(NU)) for r in range(RING)]
STEP_USES = [len(range(r, NSTREAM, RING)) for r in range(RING)]


def loads_into(ring, j, b):
    return FIRST_USES[ring] + j * STEP_USES[ring] + b // RING + 1


def entries_back(b):
    return RING if b >= RING else b + NSTREAM - max(x for x in range(NSTREAM) if x % RING == b)
FILL = (1, 1, 1, 2)
HALVES = sum(FILL)


def units_done(c, place):
    first = c * HALVES + sum(FILL[:place])
    return [h // 2 for h in range(first, first + FILL[place]) if h % 2]


def main_loop(nc, ext, d, keep):
    xn, W, ident32, stage = keep["xn"], keep["W"], keep["ident32"], keep["stage"]
    ident16, identb, neg, hot, cw, halo = (keep[k] for k in ("ident16", "identb", "neg", "hot", "cw", "halo"))
    with ExitStack() as ctx:
        def sb(name, shape, dt=F32):
            return ctx.enter_context(nc.sbuf_tensor("m_" + name, shape, dt))

        def sem(name):
            return ctx.enter_context(nc.semaphore("m_" + name))

        acc = sb("acc", [P, 2, NC, DM])
        state_in = sb("state_in", [P, GC])
        state = sb("state", [P, GC])
        st16 = sb("st16", [P, 2, GC], F16)
        raw = sb("raw", [P, 2, TAPS - 1 + ST])
        conv = sb("conv", [P, 2, ST])
        xT = sb("xT", [P, 2, XT, ST])
        bc = sb("bc", [P, 2, 2, 2, ST], F16)
        sg = sb("sg", [P, NC, GC])
        xs = sb("xs", [P, GC])
        dtx = sb("dtx", [P, GC])
        dx16 = sb("dx16", [P, 2, GC], F16)
        wx16 = sb("wx16", [P, 2, GC], F16)
        dec = sb("dec", [P, HG, P])
        g16 = sb("g16", [P, 2, HG, P], F16)
        y = sb("y", [P, GC])
        z16 = sb("z16", [P, 2, GC], F16)
        zT16 = sb("zT16", [P, 2, XT, P], F16)
        bs16 = sb("bs16", [P, 2, P], F16)
        laT = sb("laT", [NC * LAW, 2, P], BF16)
        rec = sb("rec", [P, 2, REC])
        cwg = sb("cwg", [P, CW])
        norms = sb("norms", [P, 7])
        sumsq, var, rstd, mhalf = norms[:, 0:2], norms[:, 2:4], norms[:, 4:6], norms[:, 6:7]
        ps = [ctx.enter_context(nc.psum_tensor(f"m_ps{i}", [P, 512], F32)) for i in range(8)]
        p_proj, p_out, p_x, p_misc, p_dec, p_y, p_v = ps[0:2], ps[2], ps[3], ps[4], ps[5], ps[6], ps[7]
        p_misc16 = p_misc[:].bitcast(F16)
        p_miscb = p_misc[:].bitcast(BF16)
        p_bs = p_misc16[:, 0:2 * P].rearrange("p (h n) -> p h n", h=2)
        p_la = p_miscb[:, 0:P]
        p_cb = p_misc[:, 2 * P:3 * P]
        p_zT = p_x[:].bitcast(F16).rearrange("p (h i t) -> p h i t", h=2, i=XT)

        stage_full = keep["stage_full"]
        rec_full = [sem("rec_full0"), sem("rec_full1")]
        acc_full = [sem("acc_full0"), sem("acc_full1")]
        acc_stored = [sem("acc_stored0"), sem("acc_stored1")]
        xn_full = [sem("xn_full0"), sem("xn_full1")]
        state_full, state_stored = sem("state_full"), sem("state_stored")
        proj_done, xtr_done, misc_done, dec_done, inter_done, snew_done, intra_done, ztr_done, out_done = (
            sem(n) for n in ("proj_done", "xtr_done", "misc_done", "dec_done", "inter_done", "snew_done",
                             "intra_done", "ztr_done", "out_done"))
        la_tr = sem("la_tr")
        w_high, w_split = keep["w_high"], keep["w_split"]
        proj_evac, silu_done, bc_high, xs_ready, misc_evac, dx_high, exp_done, wx_high, g_high, sq_done, z_high, st_high = (
            sem(n) for n in ("proj_evac", "silu_done", "bc_high", "xs_ready", "misc_evac", "dx_high",
                             "exp_done", "wx_high", "g_high", "sq_done", "z_high", "st_high"))
        la_ready, sg_ready = sem("la_ready"), sem("sg_ready")
        cw_ready, halo_in, conv_step, conv_done, bc_split, dtx_done, dx_split, t_done, ydx_done, wx_split, g_done, g_split, st_scaled, st_done, st_split, y_done, z_done, var_done, z_split, zt_evac, acc_done = (
            sem(n) for n in ("cw_ready", "halo_in", "conv_step", "conv_done", "bc_split", "dtx_done",
                             "dx_split", "t_done", "ydx_done", "wx_split", "g_done", "g_split", "st_scaled",
                             "st_done", "st_split", "y_done", "z_done", "var_done", "z_split", "zt_evac", "acc_done"))
        wx_done, skip_done, rstd_done, mhalf_ready = (sem(n) for n in ("wx_done", "skip_done", "rstd_done", "mhalf_ready"))
        block = ctx.enter_context(nc.Block())

        def record(s, n, c):
            o = (n * NC + c) * HG
            return rec[:, s, o:o + HG]

        def heads(ap):
            return ap.rearrange("p (h q) -> p h q", q=HD)

        def per_head(row):
            return row.unsqueeze(2).to_broadcast([P, HG, HD])

        def splits_before(j, q):
            return NU + j * NSTREAM + STREAM.index(q) + 1

        def steps(engine, body):
            body(0, False)
            with engine.Fori(1, STEPS - 1) as j:
                body(j, False)
            body(STEPS - 1, True)

        @block.sync
        def _(sp):
            def weights(n, src, ring, back):
                at_least(sp, w_split, n - back + 1)
                sp.dma_start(stage[:, ring, :], src).then_inc(stage_full[ring], 16)

            def record_in(s, j):
                if not (isinstance(j, int) and j == 0):
                    at_least(sp, z_split, 8 * j - NC * (1 - s))
                sp.dma_start(rec[:, s, :], d["rec"][:, bass.ds(2 * j + s, 1), :]).then_inc(rec_full[s], 16)

            def state_load(j, g):
                at_least(sp, st_done, 8 * (j - 1) + 1)
                sp.dma_start(state_in[:], d["state"][bass.ds(g, 1), :, :].rearrange("a p c -> p (a c)")).then_inc(state_full, 16)

            acc_view = d["part_out"].rearrange("(f s c p) n -> f s p c n", f=2, s=2, p=P)
            out_view = d["out"].rearrange("(f s c p) n -> f s p c n", f=2, s=2, p=P)
            for q in range(2 * RING, NU):
                weights(q, ext["w_proj"][0, q], (q + SHIFT) % RING, RING)
            record_in(0, 0)
            state_load(0, 0)
            record_in(1, 0)
            for s in range(2):
                sp.dma_start(acc[:, s], acc_view[0, s]).then_inc(acc_full[s], 16)

            def stream(j, g, gnext, lo, hi):
                for b in range(lo, hi):
                    q = STREAM[b]
                    src = (ext["w_out"][bass.ds(g, 1), q - NU] if q >= NU else ext["w_proj"][bass.ds(gnext, 1), q])
                    weights(NU + j * NSTREAM + b, src.rearrange("a p n -> p (a n)"), b % RING,
                            entries_back(b))

            def step(j, f, g):
                gnext = 0 if isinstance(g, int) else g + 1
                ahead = not (isinstance(j, int) and j == STEPS - 1)
                stream(j, g, gnext, 0, XT)
                if ahead:
                    stream(j, g, gnext, XT, XT + NCT)
                    record_in(0, j + 1)
                    at_least(sp, st_done, 8 * j + 1)
                    if f == 1:
                        at_least(sp, state_stored, 16 * G)
                    sp.dma_start(state_in[:], d["state"][bass.ds(gnext, 1), :, :].rearrange("a p c -> p (a c)")).then_inc(state_full, 16)
                    stream(j, g, gnext, XT + NCT, NSTREAM)
                at_least(sp, st_done, 8 * (j + 1))
                sp.dma_start(d["state"][bass.ds(g, 1), :, :].rearrange("a p c -> p (a c)"), state[:]).then_inc(state_stored, 16)
                if ahead:
                    record_in(1, j + 1)

            for f in range(2):
                with sp.Fori(0, G - 1) as g:
                    step(g + f * G, f, g)
                j = f * G + G - 1
                if f == 0:
                    stream(j, G - 1, 0, 0, XT)
                    at_least(sp, proj_done, NU * (2 * j + 1))
                    sp.dma_start(xn[:, 0].rearrange("p k h t -> p (k h t)"), d["xn"][0]).then_inc(xn_full[0], 16)
                    stream(j, G - 1, 0, XT, XT + NCT)
                    record_in(0, j + 1)
                    at_least(sp, st_done, 8 * j + 1)
                    at_least(sp, state_stored, 16 * (j + 1 - G + 0) if j + 1 - G > 0 else 16)
                    sp.dma_start(state_in[:], d["state"][0]).then_inc(state_full, 16)
                    at_least(sp, proj_done, NU * (2 * j + 2))
                    sp.dma_start(xn[:, 1].rearrange("p k h t -> p (k h t)"), d["xn"][1]).then_inc(xn_full[1], 16)
                    stream(j, G - 1, 0, XT + NCT, NSTREAM)
                    at_least(sp, acc_done, 2 * (8 * j + NC))
                    sp.dma_start(out_view[0, 0], acc[:, 0]).then_inc(acc_stored[0], 16)
                    at_least(sp, acc_stored[0], 16)
                    sp.dma_start(acc[:, 0], acc_view[1, 0]).then_inc(acc_full[0], 16)
                    at_least(sp, st_done, 8 * (j + 1))
                    sp.dma_start(d["state"][G - 1], state[:]).then_inc(state_stored, 16)
                    record_in(1, j + 1)
                    at_least(sp, acc_done, 2 * (8 * j + 8))
                    sp.dma_start(out_view[0, 1], acc[:, 1]).then_inc(acc_stored[1], 16)
                    at_least(sp, acc_stored[1], 16)
                    sp.dma_start(acc[:, 1], acc_view[1, 1]).then_inc(acc_full[1], 16)
                else:
                    stream(j, G - 1, 0, 0, XT)
                    at_least(sp, st_done, 8 * (j + 1))
                    sp.dma_start(d["state"][G - 1], state[:]).then_inc(state_stored, 16)
                    for s in range(2):
                        at_least(sp, acc_done, 2 * (8 * j + NC * (s + 1)))
                        sp.dma_start(out_view[1, s], acc[:, s]).then_inc(acc_stored[s], 16)
            at_least(sp, state_stored, 16 * STEPS)
            for s in range(2):
                at_least(sp, acc_stored[s], 32)

        @block.scalar
        def _(act):
            def split_high(j, n, q, ring, count):
                act.wait_ge(stage_full[ring], 16 * count)
                if not (isinstance(j, int) and j < 0):
                    if q < NCT:
                        at_least(act, proj_done, NU * (2 * j + 1) + q + 1)
                    elif q < NU:
                        at_least(act, proj_done, NU * (2 * j + 2))
                    else:
                        at_least(act, out_done, 2 * 8 * j)
                w = W[:, q, 0, :]
                if q < NU:
                    nc.scalar.activation(w, stage[:, ring, :], ACT.Copy, scale=SCALE).then_inc(w_high, 1)
                else:
                    nw = rec[:, 0, REC_NW + q - NU:REC_NW + q - NU + 1]
                    nc.scalar.activation(w, stage[:, ring, :], ACT.Copy, scale=nw).then_inc(w_high, 1)

            def unit_out(v, q, k):
                act.wait_ge(proj_done, NU * v + q + 1)
                if q < NCT:
                    at_least(act, conv_done, NCT * v + q - 1)
                    nc.scalar.activation(raw[:, q % 2, TAPS - 1:], p_proj[q % 2][:], ACT.Copy,
                                         scale=1.0 / SCALE).then_inc(proj_evac, 1)
                else:
                    at_least(act, z_done, NC * (v - 1) + q - NCT + 1)
                    nc.scalar.activation(sg[:, q - NCT, :], p_proj[q % 2][:], ACT.Copy,
                                         scale=1.0 / SCALE).then_inc(proj_evac, 1)

            def gate_silu(v, q):
                act.wait_ge(proj_evac, NU * v + q + 1)
                nc.scalar.activation(sg[:, q - NCT, :], sg[:, q - NCT, :], ACT.Silu).then_inc(sg_ready, 1)

            def silu(v, vp, q):
                if q >= NCT:
                    gate_silu(v, q)
                    return
                act.wait_ge(conv_done, NCT * v + q + 1)
                if q < XT:
                    if q == 0:
                        at_least(act, xtr_done, NC * (v - 1))
                    nc.scalar.activation(xT[:, vp, q, :], conv[:, q % 2, :], ACT.Silu).then_inc(silu_done, 1)
                else:
                    nc.scalar.activation(conv[:, q % 2, :], conv[:, q % 2, :], ACT.Silu).then_inc(silu_done, 1)
                    act.wait_ge(silu_done, NCT * v + q + 1)
                    if q == XT:
                        at_least(act, inter_done, NC * (v - 1))
                        at_least(act, misc_done, NC * (v - 1))
                    nc.scalar.activation(bc[:, vp, q - XT, 0, :], conv[:, q % 2, :], ACT.Copy).then_inc(bc_high, 1)

            def state_high(k, src):
                at_least(act, inter_done, k)
                nc.scalar.activation(st16[:, 0, :], src, ACT.Copy).then_inc(st_high, 1)

            def decay_exps(k, s, c, b):
                act.wait_ge(dec_done, 2 * k + b + 1)
                if b == 0:
                    at_least(act, g_split, k)
                for h in range(4):
                    i = 4 * b + h
                    last = nc.scalar.activation(dec[:, i, :], p_dec[:, h * P:(h + 1) * P], ACT.Exp,
                                                bias=record(s, A_NLA, c)[:, i:i + 1])
                last.then_inc(exp_done, 1)

            def la_out(v, vp):
                act.wait_ge(la_tr, v + 1)
                at_least(act, dec_done, 2 * NC * (v - 1))
                nc.scalar.activation(laT[:, vp, :], p_la, ACT.Copy).then_inc(la_ready, 1)

            def weights_high(j, s, c, place, last):
                for q in SPLITS.get((s, c, place), []):
                    if q >= NU or not last:
                        b = STREAM.index(q)
                        split_high(j, NU + j * NSTREAM + b, q, b % RING, loads_into(b % RING, j, b))

            for q in range(NU):
                for n in (2 * q + RING, 2 * q + RING + 1):
                    if n < NU:
                        split_high(-1, n, n, (n + SHIFT) % RING, n // RING + 1)
                if q < NCT:
                    unit_out(0, q, 0)
                if 1 <= q <= NCT:
                    silu(0, 0, q - 1)
                if q >= NCT:
                    unit_out(0, q, 0)
            la_out(0, 0)
            act.wait_ge(state_full, 16)
            state_high(0, state_in[:])
            for q in (NCT, NCT + 1):
                gate_silu(0, q)
            act.wait_ge(rec_full[0], 16)
            decay_exps(0, 0, 0, 0)

            def body(j, last):
                for s in range(2):
                    ahead = not (last and s == 1)
                    v = 2 * j + s
                    for c in range(NC):
                        k = 8 * j + NC * s + c
                        units = lambda place: units_done(c, place) if ahead else []
                        silus = lambda which: which.get(c, []) if ahead else []
                        act.wait_ge(xtr_done, k + 1)
                        at_least(act, z_split, k)
                        nc.scalar.activation(xs[:], p_x[:], ACT.Copy).then_inc(xs_ready, 1)
                        act.wait_ge(misc_done, k + 1)
                        at_least(act, snew_done, k)
                        nc.scalar.activation(bs16[:], p_bs, ACT.Copy).then_inc(misc_evac, 1)
                        act.wait_ge(dtx_done, k + 1)
                        at_least(act, intra_done, k)
                        nc.scalar.activation(dx16[:, 0, :], dtx[:], ACT.Copy).then_inc(dx_high, 1)
                        decay_exps(k, s, c, 1)
                        weights_high(j, s, c, 0, last)
                        for q in units(0):
                            unit_out(v + 1, q, k)
                        act.wait_ge(wx_done, k + 1)
                        at_least(act, snew_done, k)
                        nc.scalar.activation(wx16[:, 0, :], dtx[:], ACT.Copy).then_inc(wx_high, 1)
                        act.wait_ge(g_done, k + 1)
                        at_least(act, intra_done, k)
                        nc.scalar.activation(g16[:, 0], dec[:], ACT.Copy).then_inc(g_high, 1)
                        for q in units(1):
                            unit_out(v + 1, q, k)
                        for q in [NU - 2, NU - 1] if c == 0 else []:
                            gate_silu(v, q)
                        for q in silus(SILU_MID):
                            silu(v + 1, (s + 1) % 2, q)
                        if not (last and s == 1 and c == NC - 1):
                            act.wait_ge(st_done, k + 1)
                            if s == 1 and c == NC - 1:
                                act.wait_ge(state_full, 16 * (j + 2))
                                state_high(k + 1, state_in[:])
                            else:
                                state_high(k + 1, state[:])
                        for q in units(2):
                            unit_out(v + 1, q, k)
                        act.wait_ge(y_done, k + 1)
                        at_least(act, ztr_done, k)
                        nc.scalar.activation(z16[:, 1, :], y[:], ACT.Square, accum_out=sumsq[:, c % 2:c % 2 + 1]).then_inc(sq_done, 1)
                        act.wait_ge(z_done, k + 1)
                        nc.scalar.activation(z16[:, 0, :], xs[:], ACT.Copy).then_inc(z_high, 1)
                        weights_high(j, s, c, 1, last)
                        for q in silus(SILU_END):
                            silu(v + 1, (s + 1) % 2, q)
                        if c == NC - 2 and ahead:
                            la_out(v + 1, 1 - s)
                        if c == NC - 1 and ahead:
                            act.wait_ge(rec_full[1 - s], 16 * (j + 1) if s == 0 else 16 * (j + 2))
                        if c < NC - 1 or ahead:
                            decay_exps(k + 1, s if c < NC - 1 else 1 - s, (c + 1) % NC, 0)
                        for q in units(3):
                            unit_out(v + 1, q, k)

            steps(act, body)

        @block.gpsimd
        def _(pool):
            nc.gpsimd.memset(mhalf, LN_POW).then_inc(mhalf_ready, 1)
            pool.wait_ge(mhalf_ready, 1)

            def body(j, last):
                for s in range(2):
                    for c in range(NC):
                        k = 8 * j + NC * s + c
                        if c == 0:
                            pool.wait_ge(rec_full[s], 16 * (j + 1))
                        pool.wait_ge(dx_split, k + 1)
                        nc.gpsimd.tensor_tensor(heads(dtx[:]), heads(dtx[:]), per_head(record(s, A_W, c)),
                                                ALU.mult).then_inc(wx_done, 1)
                        nc.gpsimd.tensor_tensor(heads(xs[:]), heads(xs[:]), per_head(rec[:, s, REC_D:REC_D + HG]),
                                                ALU.mult).then_inc(skip_done, 1)
                        pool.wait_ge(var_done, k + 1)
                        at_least(pool, acc_done, 2 * (k - 1))
                        nc.gpsimd.tensor_tensor(rstd[:, c % 2:c % 2 + 1], var[:, c % 2:c % 2 + 1], mhalf,
                                                ALU.pow).then_inc(rstd_done, 1)

            steps(pool, body)

        @block.vector
        def _(dve):
            def split_low(q, ring, n):
                dve.wait_ge(w_high, n + 1)
                sc = SCALE if q < NU else rec[:, 0, REC_NW + q - NU:REC_NW + q - NU + 1]
                nc.vector.scalar_tensor_tensor(W[:, q, 1, :], stage[:, ring, :], sc, W[:, q, 0, :],
                                               op0=ALU.mult, op1=ALU.subtract).then_inc(w_split, 1)

            def weights_low(j, s, c, place, last):
                for q in SPLITS.get((s, c, place), []):
                    if q >= NU or not last:
                        b = STREAM.index(q)
                        split_low(q, b % RING, NU + j * NSTREAM + b)

            def group_constants(j):
                at_least(dve, conv_done, 2 * NCT * j)
                g = j % G
                nc.vector.tensor_copy(cwg[:], cw[:, bass.ds(g * CW, CW)]).then_inc(cw_ready, 1)
                dve.wait_ge(cw_ready, j + 1)

            def convolve(j, s, q):
                v = 2 * j + s
                o = q * (TAPS + 1)
                n = TAPS - 1
                r = raw[:, q % 2, :]
                a = conv[:, q % 2, :]
                w = lambda t: cwg[:, o + t:o + t + 1]
                carried = halo[:, bass.ds((j % G) * NCT * n + q * n, n)]
                dve.wait_ge(proj_evac, NU * v + q + 1)
                at_least(dve, silu_done, NCT * v + q - 1)
                if q >= XT:
                    at_least(dve, bc_split, 2 * v)
                nc.vector.tensor_copy(r[:, 0:n], carried).then_inc(halo_in, 1)
                nc.vector.tensor_scalar(a, r[:, n:n + ST], w(n), w(TAPS), ALU.mult, ALU.add).then_inc(conv_step, 1)
                dve.wait_ge(halo_in, NCT * v + q + 1)
                for t in range(n - 1, -1, -1):
                    dve.wait_ge(conv_step, n * (NCT * v + q) + n - t)
                    last = nc.vector.scalar_tensor_tensor(a, r[:, t:t + ST], w(t), a, op0=ALU.mult, op1=ALU.add)
                    if t:
                        last.then_inc(conv_step, 1)
                nc.vector.tensor_copy(carried, r[:, ST:ST + n]).then_inc(conv_done, 1)

            def bc_low(v, vp, q):
                dve.wait_ge(bc_high, 2 * v + q - XT + 1)
                nc.vector.tensor_tensor(bc[:, vp, q - XT, 1, :], conv[:, q % 2, :], bc[:, vp, q - XT, 0, :],
                                        ALU.subtract).then_inc(bc_split, 1)

            def state_low(k, src):
                dve.wait_ge(st_high, k + 1)
                nc.vector.tensor_tensor(st16[:, 1, :], src, st16[:, 0, :], ALU.subtract).then_inc(st_split, 1)

            def zt_out(k):
                dve.wait_ge(ztr_done, k + 1)
                at_least(dve, out_done, 2 * k)
                nc.vector.tensor_copy(zT16[:], p_zT).then_inc(zt_evac, 1)

            def add_out(k, b, s, c):
                dve.wait_ge(out_done, 2 * k + b + 1)
                if b == 0:
                    dve.wait_ge(rstd_done, k + 1)
                o = acc[:, s, c, b * 512:(b + 1) * 512]
                nc.vector.scalar_tensor_tensor(o, p_out[:], rstd[:, c % 2:c % 2 + 1], o, op0=ALU.mult,
                                               op1=ALU.add).then_inc(acc_done, 1)

            group_constants(0)
            for q in range(NU):
                for n in (2 * q + RING, 2 * q + RING + 1):
                    if n < NU:
                        split_low(n, (n + SHIFT) % RING, n)
                if q < NCT:
                    convolve(0, 0, q)
                if XT + 1 <= q <= XT + 2:
                    bc_low(0, 0, q - 1)
            state_low(0, state_in[:])

            def body(j, last):
                for s in range(2):
                    ahead = not (last and s == 1)
                    v = 2 * j + s
                    nj, ns = (j, 1) if s == 0 else (j + 1, 0)
                    for c in range(NC):
                        k = 8 * j + NC * s + c
                        first = isinstance(k, int) and k == 0
                        ps_, pc = ((s, c - 1) if c else (1 - s, NC - 1))
                        if c == 0:
                            dve.wait_ge(rec_full[s], 16 * (j + 1))
                            if s == 1 and ahead:
                                group_constants(j + 1)
                        dve.wait_ge(xs_ready, k + 1)
                        at_least(dve, wx_split, k)
                        nc.vector.tensor_tensor(heads(dtx[:]), heads(xs[:]), per_head(record(s, A_DT, c)),
                                                ALU.mult).then_inc(dtx_done, 1)
                        dve.wait_ge(dx_high, k + 1)
                        nc.vector.tensor_tensor(dx16[:, 1, :], dtx[:], dx16[:, 0, :], ALU.subtract).then_inc(dx_split, 1)
                        dve.wait_ge(inter_done, k + 1)
                        at_least(dve, sq_done, k)
                        nc.vector.tensor_tensor(heads(y[:]), heads(p_v[:]), per_head(record(s, A_ELA, c)),
                                                ALU.mult).then_inc(t_done, 1)
                        if not first:
                            zt_out(k - 1)
                        weights_low(j, s, c, 0, last)
                        dve.wait_ge(exp_done, 2 * k + 2)
                        nc.vector.tensor_tensor(dec[:], dec[:], p_cb.unsqueeze(1).to_broadcast([P, HG, P]),
                                                ALU.mult).then_inc(g_done, 1)
                        dve.wait_ge(wx_high, k + 1)
                        nc.vector.tensor_tensor(wx16[:, 1, :], dtx[:], wx16[:, 0, :], ALU.subtract).then_inc(wx_split, 1)
                        dve.wait_ge(skip_done, k + 1)
                        dve.wait_ge(t_done, k + 1)
                        nc.vector.tensor_tensor(y[:], y[:], xs[:], ALU.add).then_inc(ydx_done, 1)
                        dve.wait_ge(g_high, k + 1)
                        nc.vector.tensor_tensor(g16[:, 1], dec[:], g16[:, 0], ALU.subtract).then_inc(g_split, 1)
                        if not first:
                            if c == 1:
                                dve.wait_ge(acc_full[s], 16 * (j // G + 1))
                            add_out(k - 1, 0, ps_, pc)
                        src = state_in if s == 0 and c == 0 else state
                        if s == 0 and c == 0:
                            at_least(dve, state_stored, 16 * j)
                        nc.vector.tensor_tensor(heads(state[:]), heads(src[:]), per_head(record(s, A_ETOT, c)),
                                                ALU.mult).then_inc(st_scaled, 1)
                        for q in units_done(c - 1, 3) if ahead and c else []:
                            if q < NCT:
                                convolve(nj, ns, q)
                        dve.wait_ge(snew_done, k + 1)
                        dve.wait_ge(st_scaled, k + 1)
                        nc.vector.tensor_tensor(state[:], state[:], p_v[:], ALU.add).then_inc(st_done, 1)
                        if not first:
                            add_out(k - 1, 1, ps_, pc)
                        if not (last and s == 1 and c == NC - 1):
                            dve.wait_ge(st_done, k + 1)
                            state_low(k + 1, state_in[:] if (s == 1 and c == NC - 1) else state[:])
                        dve.wait_ge(intra_done, k + 1)
                        dve.wait_ge(ydx_done, k + 1)
                        nc.vector.tensor_tensor(y[:], y[:], p_y[:], ALU.add).then_inc(y_done, 1)
                        if c == 0:
                            dve.wait_ge(sg_ready, NC * v + 2)
                        elif c == 2:
                            dve.wait_ge(sg_ready, NC * v + NC)
                        dve.wait_ge(y_done, k + 1)
                        nc.vector.scalar_tensor_tensor(xs[:], y[:], SCALE, sg[:, c, :], op0=ALU.mult,
                                                       op1=ALU.mult).then_inc(z_done, 1)
                        dve.wait_ge(sq_done, k + 1)
                        at_least(dve, rstd_done, k - 1)
                        nc.vector.tensor_scalar(var[:, c % 2:c % 2 + 1], sumsq[:, c % 2:c % 2 + 1], OUT_POW2 / GC,
                                                EPS * OUT_POW2, ALU.mult, ALU.add).then_inc(var_done, 1)
                        dve.wait_ge(z_high, k + 1)
                        nc.vector.tensor_tensor(z16[:, 1, :], xs[:], z16[:, 0, :], ALU.subtract).then_inc(z_split, 1)
                        for q in units_done(c, 0) + units_done(c, 1) + units_done(c, 2) if ahead else []:
                            if q < NCT:
                                convolve(nj, ns, q)
                        weights_low(j, s, c, 1, last)
                        if ahead and c >= 2:
                            bc_low(v + 1, (s + 1) % 2, XT + c - 2)

            steps(dve, body)
            zt_out(STEPS * 8 - 1)
            for b in range(2):
                add_out(STEPS * 8 - 1, b, 1, NC - 1)

        @block.tensor
        def _(pe):
            def three(out, lhs, rhs, first, stop):
                for n, (a, b) in enumerate(((0, 0), (0, 1), (1, 0))):
                    last = nc.tensor.matmul(out, lhs(a), rhs(b), start=first and n == 0, stop=stop and n == 2)
                return last

            def half_unit(v, vp, h, ready):
                q, part = h // 2, h % 2
                out = p_proj[q % 2][:]
                if part == 0:
                    at_least(pe, proj_evac, NU * v + q - 1)
                    at_least(pe, w_split, ready(min(q, NCT) if q < NCT else NU - 1))
                for k in range(4 * part, 4 * part + 4):
                    if q < NCT:
                        last = three(out, lambda x: W[:, q, x, k * P:(k + 1) * P], lambda x: xn[:, vp, k, x, :],
                                     k == 0, k == KT - 1)
                    else:
                        t = (q - NCT) * P
                        last = three(out, lambda x: xn[:, vp, k, x, t:t + P],
                                     lambda x: W[:, NCT + k // 2, x, (k % 2) * 512:(k % 2 + 1) * 512],
                                     k == 0, k == KT - 1)
                if part:
                    last.then_inc(proj_done, 1)

            def out_half(k, b, fresh=None):
                at_least(pe, acc_done, 2 * k + b)
                for i in range(XT):
                    if fresh is not None:
                        pe.wait_ge(w_split, splits_before(fresh, NU + i))
                    last = three(p_out[:], lambda x: zT16[:, x, i, :],
                                 lambda x: W[:, NU + i, x, b * 512:(b + 1) * 512], i == 0, i == XT - 1)
                last.then_inc(out_done, 1)

            def gated_transposes(k):
                pe.wait_ge(z_split, k + 1)
                for x in range(2):
                    for i in range(XT):
                        last = nc.tensor.transpose(p_zT[:, x, i, :], z16[:, x, i * P:(i + 1) * P], ident16[:])
                last.then_inc(ztr_done, 1)

            def la_transpose(v, s, arrived):
                pe.wait_ge(rec_full[s], arrived)
                at_least(pe, g_done, NC * v - 1)
                nc.tensor.transpose(p_la, rec[:, s, REC_LA:REC].bitcast(BF16), identb[:]).then_inc(la_tr, 1)

            def decays(k, v, s, c, b):
                if b == 0 and c == 0:
                    pe.wait_ge(la_ready, v + 1)
                at_least(pe, exp_done, 2 * k + b)
                nc.tensor.matmul(p_dec[:], identb[:], neg[:].unsqueeze(1).to_broadcast([P, 4, P]), start=True, stop=False)
                rows = slice(c * LAW, (c + 1) * LAW)
                for h in range(4):
                    i = 4 * b + h
                    last = nc.tensor.matmul(p_dec[:, h * P:(h + 1) * P], hot[rows, i * P:(i + 1) * P], laT[rows, s, :],
                                            start=False, stop=h == 3)
                last.then_inc(dec_done, 1)

            for h in range(2 * NU):
                half_unit(0, 0, h, lambda q: q + 1)
            la_transpose(0, 0, 16)
            decays(0, 0, 0, 0, 0)

            def body(j, last_step):
                for s in range(2):
                    ahead = not (last_step and s == 1)
                    v = 2 * j + s
                    ready = (lambda q: NU if isinstance(j, int) and j == 0 else splits_before(j - 1, q)) if s == 0 else (
                        lambda q: splits_before(j, q))
                    for c in range(NC):
                        k = 8 * j + NC * s + c
                        first = isinstance(k, int) and k == 0
                        t = slice(c * P, (c + 1) * P)

                        def fill(place, lo=0, hi=9):
                            if ahead:
                                h0 = c * HALVES + sum(FILL[:place])
                                for h in range(h0 + lo, h0 + min(FILL[place], hi)):
                                    if h == 0:
                                        at_least(pe, xn_full[1 - s], 16 * ((j if s == 0 else j + 1) // G))
                                    half_unit(v + 1, 1 - s, h, ready)

                        if c == 0:
                            pe.wait_ge(silu_done, NCT * v + XT)
                        at_least(pe, zt_evac, k - 1)
                        for i in range(XT):
                            last = nc.tensor.transpose(p_x[:, i * P:(i + 1) * P], xT[:, s, i, t], ident32[:])
                        last.then_inc(xtr_done, 1)
                        if c == 0:
                            pe.wait_ge(bc_split, 2 * (v + 1))
                        if c == NC - 1 and ahead:
                            pe.wait_ge(la_ready, v + 2)
                        elif c == 0:
                            pe.wait_ge(la_ready, v + 1)
                        at_least(pe, g_done, k)
                        for x in range(2):
                            nc.tensor.transpose(p_bs[:, x, :], bc[:, s, 0, x, t], ident16[:])
                        three(p_cb, lambda x: bc[:, s, 0, x, t], lambda x: bc[:, s, 1, x, t], True, True).then_inc(misc_done, 1)
                        fill(0)

                        decays(k, v, s, c, 1)
                        pe.wait_ge(misc_evac, k + 1)
                        pe.wait_ge(st_split, k + 1)
                        at_least(pe, st_done, k)
                        three(p_v[:], lambda x: bc[:, s, 1, x, t], lambda x: st16[:, x, :], True, True).then_inc(inter_done, 1)
                        if not first:
                            pe.wait_ge(xs_ready, k + 1)
                            gated_transposes(k - 1)
                        fill(1)
                        if not first:
                            pe.wait_ge(zt_evac, k)
                            out_half(k - 1, 0, j if s == 0 and c == 1 else None)
                        pe.wait_ge(t_done, k + 1)
                        pe.wait_ge(wx_split, k + 1)
                        three(p_v[:], lambda x: bs16[:, x, :], lambda x: wx16[:, x, :], True, True).then_inc(snew_done, 1)
                        fill(2)
                        if not first:
                            out_half(k - 1, 1)
                        pe.wait_ge(g_split, k + 1)
                        pe.wait_ge(dx_split, k + 1)
                        at_least(pe, y_done, k)
                        for h in range(HG):
                            o = slice(h * HD, (h + 1) * HD)
                            last = three(p_y[:, o], lambda x: g16[:, x, h, :], lambda x: dx16[:, x, o], True, True)
                        last.then_inc(intra_done, 1)
                        if c == NC - 2 and ahead:
                            la_transpose(v + 1, 1 - s, 16 * (j + 1) if s == 0 else 16 * (j + 2))
                        if c < NC - 1:
                            decays(k + 1, v, s, c + 1, 0)
                        elif ahead:
                            decays(k + 1, v + 1, 1 - s, 0, 0)
                        fill(3)

            steps(pe, body)
            gated_transposes(STEPS * 8 - 1)
            pe.wait_ge(zt_evac, STEPS * 8)
            for b in range(2):
                out_half(STEPS * 8 - 1, b)


def layer(nc, ext, out):
    d = {
        "xn": nc.dram_tensor("xn_scratch", [2, P, KT * 2 * ST], F16).ap(),
        "rec": nc.dram_tensor("rec_scratch", [P, 2 * STEPS, REC], F32).ap(),
        "state": nc.dram_tensor("state_scratch", [G, P, GC], F32).ap(),
        "part_out": nc.dram_tensor("part_scratch", [L, DM], F32).ap(),
        "out": out,
    }
    with ExitStack() as ctx:
        def sb(name, shape, dt=F32):
            return ctx.enter_context(nc.sbuf_tensor(name, shape, dt))

        keep = {
            "xn": sb("xn_hl", [P, 2, KT, 2, ST], F16),
            "W": sb("W_hl", [P, NU + XT, 2, DM], F16),
            "stage": sb("stage_w", [P, RING, DM]),
            "ident32": sb("ident32", [P, P]),
            "ident16": sb("ident16", [P, P], F16),
            "identb": sb("identb", [P, P], BF16),
            "neg": sb("neg", [P, P], BF16),
            "hot": sb("hot", [P, HG * P], BF16),
            "cw": sb("cw", [P, G * CW]),
            "halo": sb("halo", [P, G * NCT * (TAPS - 1)]),
            "s_chain": ctx.enter_context(nc.semaphore("s_chain")),
            "stage_full": [ctx.enter_context(nc.semaphore(f"stage_full{r}")) for r in range(RING)],
            "w_high": ctx.enter_context(nc.semaphore("w_high")),
            "w_split": ctx.enter_context(nc.semaphore("w_split")),
        }
        prologue(nc, ext, d, keep)
        main_loop(nc, ext, d, keep)


def kernel(**inputs):
    import numpy as np
    import concourse.bacc as bacc
    from concourse.bass_utils import run_bass_kernel_spmd

    a = {k.removeprefix("L0_"): np.asarray(v) for k, v in inputs.items()}
    I = H * HD
    w = a["attn_in_proj_w"]

    def k_major(rows):
        return rows.T.reshape(KT, P, -1).transpose(1, 0, 2)

    proj, conv = [], []
    cw = np.concatenate([a["attn_conv_weight"], a["attn_conv_bias"][:, None]], 1)
    for g in range(G):
        chans = [g * GC + i * P for i in range(XT)] + [I + g * NS, I + G * NS + g * NS]
        proj += [k_major(w[I + o:I + o + P]).reshape(P, -1) for o in chans]
        gate = k_major(w[g * GC:(g + 1) * GC])
        proj += [gate[:, 2 * i:2 * i + 2].reshape(P, -1) for i in range(4)]
        conv += [cw[o:o + P] for o in chans]
    aux = np.concatenate([w[-H:], a["ffn_W_router"], a["ffn_lora_A"].transpose(0, 2, 1).reshape(ER, DM)], 0)
    aux = k_major(aux).reshape(P, 2, 4 * AUX).transpose(1, 0, 2)
    r = np.arange(P)
    cst = np.zeros((P, CST), np.float32)
    cst[:, C_ID:C_ID + P] = np.eye(P)
    cst[:, C_LE:C_LE + P] = r[:, None] <= r[None, :]
    cst[:, C_GT:C_GT + P] = r[:, None] > r[None, :]
    cst[:, C_NEG:C_NEG + P] = np.where(r[:, None] > r[None, :], -1e38, 0.0)
    for n in range(PARTS):
        for h in range(HG):
            for c in range(NC):
                cst[c * LAW + n * HG + h, C_HOT + h * P:C_HOT + (h + 1) * P] = 1
    cst[:, C_K:] = np.arange(1, E + 1)
    arrays = {
        "x": a["attn_hidden_states"].reshape(L, DM),
        "w_proj": np.stack(proj).reshape(G, NU, P, DM),
        "w_out": a["attn_out_proj_w"].T.reshape(G, XT, P, DM),
        "conv": np.stack(conv).reshape(G * NCT, P, TAPS + 1).transpose(1, 0, 2).reshape(P, G * CW),
        "norm_w": a["attn_norm_weight"].reshape(G * XT, P).T,
        "dt_bias": a["attn_dt_bias"][None], "A_log": a["attn_A_log"][None], "D": a["attn_D"][None],
        "w_base": a["ffn_W_base"].T.reshape(KT, P, DM), "w_aux": aux,
        "b_base": a["ffn_b_base"][None], "b_router": a["ffn_b_router"][None],
        "lora_B": a["ffn_lora_B"].reshape(ER, DM), "cst": cst,
    }
    arrays = {"in_" + k: np.ascontiguousarray(v) for k, v in arrays.items()}
    nc = bacc.Bacc("TRN2", target_bir_lowering=False, num_devices=1)
    ext = {k[3:]: nc.dram_tensor(k, v.shape, mybir.dt.from_np(v.dtype), kind="ExternalInput").ap() for k, v in arrays.items()}
    out = nc.dram_tensor("out_0", (L, DM), F32, kind="ExternalOutput").ap()
    layer(nc, ext, out)
    res = run_bass_kernel_spmd(nc, [arrays], core_ids=[0])
    return res.results[0]["out_0"].reshape(1, L, DM)
```
